# Optimizing a Trainium2 kernel written in Bass

```python
import numpy as np
import jax
import jax.numpy as jnp

def _softmax(x, axis=-1):
    return jax.nn.softmax(x, axis=axis)

def _gelu(x):
    return jax.nn.gelu(x, approximate=True)

def _silu(x):
    return jax.nn.silu(x)

def _sigmoid(x):
    return jax.nn.sigmoid(x)

def _layernorm(x, axis=-1, eps=1e-05):
    m = jnp.mean(x, axis=axis, keepdims=True)
    v = jnp.var(x, axis=axis, keepdims=True)
    return (x - m) / jnp.sqrt(v + eps)

def _scatter_add(tgt, idx, src, axis=0):
    return tgt.at[idx].add(src)

def _segment_sum(src, seg, n):
    return jax.ops.segment_sum(src, seg, n)
kernel_name = 'mk_metaformer_d2_conv_nhwc768_r2_f59fe3'

def setup_inputs(seed: int=0):
    np.random.seed(seed)
    _w = jnp.asarray

    def _rec_inputs():
        import jax
        import jax.numpy as jnp
        _gk = jax.random.key(seed)
        x = -0.0005963 + 1.001 * jax.random.normal(jax.random.fold_in(_gk, 1), (1, 32, 32, 384), jnp.float32)
        return x
    x = _rec_inputs()

    def _L0_conv_setup():
        import jax, jax.numpy as jnp
        import numpy as np
        NUM_HEADS = 12
        key = jax.random.key(seed)
        k1, k2, k3 = jax.random.split(key, 3)
        dim = 384
        x = jax.random.normal(k1, (1, 32, 32, dim), dtype=jnp.float32)
        qkv_w = jax.random.normal(k2, (3 * dim, dim), dtype=jnp.float32) * dim ** (-0.5)
        qkv_b = jnp.zeros((3 * dim,), dtype=jnp.float32)
        proj_w = jax.random.normal(k3, (dim, dim), dtype=jnp.float32) * dim ** (-0.5)
        proj_b = jnp.zeros((dim,), dtype=jnp.float32)
        return {'x': x, 'qkv_w': qkv_w, 'qkv_b': qkv_b, 'proj_w': proj_w, 'proj_b': proj_b}
    _L0_conv_all = _L0_conv_setup()
    _L0_conv_in = {k: v for k, v in _L0_conv_all.items() if k in ('qkv_w', 'qkv_b', 'proj_w', 'proj_b')}
    del _L0_conv_all

    def _L0_ffn_setup():
        import jax, jax.numpy as jnp
        import numpy as np
        N_EMBD = 384
        HIDDEN = 4 * N_EMBD
        N_EXPERTS = 8
        TOP_K = 2
        key = jax.random.key(seed)
        ks = jax.random.split(key, 4)
        B, T, C, E, H = (4, 1024, N_EMBD, N_EXPERTS, HIDDEN)
        x = jax.random.normal(ks[0], (B, T, C), dtype=jnp.float32)
        gate_w = jax.random.normal(ks[1], (E, C), dtype=jnp.float32) * 0.02
        gate_b = jnp.zeros((E,), dtype=jnp.float32)
        w_fc = jax.random.normal(ks[2], (E, H, C), dtype=jnp.float32) * 0.02
        b_fc = jnp.zeros((E, H), dtype=jnp.float32)
        w_proj = jax.random.normal(ks[3], (E, C, H), dtype=jnp.float32) * 0.02
        b_proj = jnp.zeros((E, C), dtype=jnp.float32)
        return {'x': x, 'gate_w': gate_w, 'gate_b': gate_b, 'w_fc': w_fc, 'b_fc': b_fc, 'w_proj': w_proj, 'b_proj': b_proj}
    _L0_ffn_all = _L0_ffn_setup()
    _L0_ffn_in = {k: v for k, v in _L0_ffn_all.items() if k in ('gate_w', 'gate_b', 'w_fc', 'b_fc', 'w_proj', 'b_proj')}
    del _L0_ffn_all

    def _L1_conv_setup():
        import jax, jax.numpy as jnp
        import numpy as np
        D_MODEL = 384
        N_HEADS = 12
        HEAD_DIM = D_MODEL // N_HEADS
        FFN_DIM = 1536
        MAX_WAVELENGTH = 10000.0
        ROPE_PERCENT = 0.5
        NORM_EPS = 1e-05

        def _layernorm(x, g, b):
            mu = jnp.mean(x, axis=-1, keepdims=True)
            var = jnp.mean(jnp.square(x - mu), axis=-1, keepdims=True)
            return (x - mu) * jax.lax.rsqrt(var + NORM_EPS) * g + b

        def _apply_p_rope(x, positions):
            half = HEAD_DIM // 2
            rope_angles = int(ROPE_PERCENT * HEAD_DIM) // 2
            fraction = 2.0 * jnp.arange(rope_angles, dtype=jnp.float32) / HEAD_DIM
            timescale = jnp.concatenate([MAX_WAVELENGTH ** fraction, jnp.full((half - rope_angles,), jnp.inf, dtype=jnp.float32)])
            angles = positions[:, None].astype(jnp.float32) / timescale[None, :]
            sin = jnp.sin(angles)[None, None]
            cos = jnp.cos(angles)[None, None]
            x1, x2 = jnp.split(x, 2, axis=-1)
            return jnp.concatenate([x1 * cos - x2 * sin, x2 * cos + x1 * sin], axis=-1)

        def _forward(hidden_state, wq, bq, wk, bk, wv, bv, wo, bo, attn_biases, ln1_g, ln1_b, ln3_g, ln3_b, w1, b1, w2, b2):
            B, C, S, D = hidden_state.shape
            T = C * S
            flat = hidden_state.reshape(B, T, D)
            ni = _layernorm(flat, ln1_g, ln1_b)
            scaling = HEAD_DIM ** (-0.5)
            q = (ni @ wq + bq) * scaling
            k = ni @ wk + bk
            v = ni @ wv + bv
            to_heads = lambda t: t.reshape(B, T, N_HEADS, HEAD_DIM).transpose(0, 2, 1, 3)
            q, k, v = (to_heads(q), to_heads(k), to_heads(v))
            positions = jnp.arange(T)
            k = _apply_p_rope(k, positions)
            q = _apply_p_rope(q, positions)
            scores = jnp.einsum('bhtd,bhsd->bhts', q, k)
            variate_ids = positions // S
            same = (variate_ids[:, None] == variate_ids[None, :]).astype(scores.dtype)
            variate_bias = same[None, :, :] * attn_biases[:, 0][:, None, None] + (1.0 - same[None, :, :]) * attn_biases[:, 1][:, None, None]
            scores = scores + variate_bias[None]
            probs = jax.nn.softmax(scores, axis=-1)
            attn = jnp.einsum('bhts,bhsd->bhtd', probs, v)
            attn = attn.transpose(0, 2, 1, 3).reshape(B, T, D)
            attn = attn @ wo + bo
            flat = flat + attn
            ff_in = _layernorm(flat, ln3_g, ln3_b)
            ff = jax.nn.gelu(ff_in @ w1 + b1, approximate=False) @ w2 + b2
            flat = flat + ff
            return flat.reshape(B, C, S, D)
        key = jax.random.key(seed)
        ks = jax.random.split(key, 12)
        B, C, S = (2, 16, 64)
        init = lambda k, shape: jax.random.normal(k, shape, dtype=jnp.float32) * 0.02
        return {'hidden_state': jax.random.normal(ks[0], (B, C, S, D_MODEL), dtype=jnp.float32), 'wq': init(ks[1], (D_MODEL, D_MODEL)), 'bq': jnp.zeros((D_MODEL,), jnp.float32), 'wk': init(ks[2], (D_MODEL, D_MODEL)), 'bk': jnp.zeros((D_MODEL,), jnp.float32), 'wv': init(ks[3], (D_MODEL, D_MODEL)), 'bv': jnp.zeros((D_MODEL,), jnp.float32), 'wo': init(ks[4], (D_MODEL, D_MODEL)), 'bo': jnp.zeros((D_MODEL,), jnp.float32), 'attn_biases': init(ks[5], (N_HEADS, 2)), 'ln1_g': jnp.ones((D_MODEL,), jnp.float32), 'ln1_b': jnp.zeros((D_MODEL,), jnp.float32), 'ln3_g': jnp.ones((D_MODEL,), jnp.float32), 'ln3_b': jnp.zeros((D_MODEL,), jnp.float32), 'w1': init(ks[6], (D_MODEL, FFN_DIM)), 'b1': jnp.zeros((FFN_DIM,), jnp.float32), 'w2': init(ks[7], (FFN_DIM, D_MODEL)), 'b2': jnp.zeros((D_MODEL,), jnp.float32)}
    _L1_conv_all = _L1_conv_setup()
    _L1_conv_in = {k: v for k, v in _L1_conv_all.items() if k in ('wq', 'bq', 'wk', 'bk', 'wv', 'bv', 'wo', 'bo', 'attn_biases', 'ln1_g', 'ln1_b', 'ln3_g', 'ln3_b', 'w1', 'b1', 'w2', 'b2')}
    del _L1_conv_all

    def _L1_ffn_setup():
        import jax, jax.numpy as jnp
        import numpy as np
        B, S, H, F, E = (8, 256, 384, 1536, 6)
        TOP_K = 2
        key = jax.random.key(seed)
        ks = jax.random.split(key, 7)
        sH = 1.0 / np.sqrt(H)
        sF = 1.0 / np.sqrt(F)
        return {'x': jax.random.normal(ks[0], (B, S, H), dtype=jnp.float32), 'gate_w': jax.random.normal(ks[1], (H, E), dtype=jnp.float32) * sH, 'gate_b': jax.random.normal(ks[2], (E,), dtype=jnp.float32) * 0.01, 'w1': jax.random.normal(ks[3], (E, H, F), dtype=jnp.float32) * sH, 'b1': jax.random.normal(ks[4], (E, F), dtype=jnp.float32) * 0.01, 'w2': jax.random.normal(ks[5], (E, F, H), dtype=jnp.float32) * sF, 'b2': jax.random.normal(ks[6], (E, H), dtype=jnp.float32) * 0.01}
    _L1_ffn_all = _L1_ffn_setup()
    _L1_ffn_in = {k: v for k, v in _L1_ffn_all.items() if k in ('gate_w', 'gate_b', 'w1', 'b1', 'w2', 'b2')}
    del _L1_ffn_all
    return {'x': x, 'L0_conv_qkv_w': _L0_conv_in['qkv_w'], 'L0_conv_qkv_b': _L0_conv_in['qkv_b'], 'L0_conv_proj_w': _L0_conv_in['proj_w'], 'L0_conv_proj_b': _L0_conv_in['proj_b'], 'L0_ffn_gate_w': _L0_ffn_in['gate_w'], 'L0_ffn_gate_b': _L0_ffn_in['gate_b'], 'L0_ffn_w_fc': _L0_ffn_in['w_fc'], 'L0_ffn_b_fc': _L0_ffn_in['b_fc'], 'L0_ffn_w_proj': _L0_ffn_in['w_proj'], 'L0_ffn_b_proj': _L0_ffn_in['b_proj'], 'L1_conv_wq': _L1_conv_in['wq'], 'L1_conv_bq': _L1_conv_in['bq'], 'L1_conv_wk': _L1_conv_in['wk'], 'L1_conv_bk': _L1_conv_in['bk'], 'L1_conv_wv': _L1_conv_in['wv'], 'L1_conv_bv': _L1_conv_in['bv'], 'L1_conv_wo': _L1_conv_in['wo'], 'L1_conv_bo': _L1_conv_in['bo'], 'L1_conv_attn_biases': _L1_conv_in['attn_biases'], 'L1_conv_ln1_g': _L1_conv_in['ln1_g'], 'L1_conv_ln1_b': _L1_conv_in['ln1_b'], 'L1_conv_ln3_g': _L1_conv_in['ln3_g'], 'L1_conv_ln3_b': _L1_conv_in['ln3_b'], 'L1_conv_w1': _L1_conv_in['w1'], 'L1_conv_b1': _L1_conv_in['b1'], 'L1_conv_w2': _L1_conv_in['w2'], 'L1_conv_b2': _L1_conv_in['b2'], 'L1_ffn_gate_w': _L1_ffn_in['gate_w'], 'L1_ffn_gate_b': _L1_ffn_in['gate_b'], 'L1_ffn_w1': _L1_ffn_in['w1'], 'L1_ffn_b1': _L1_ffn_in['b1'], 'L1_ffn_w2': _L1_ffn_in['w2'], 'L1_ffn_b2': _L1_ffn_in['b2']}

def reference(x, L0_conv_qkv_w, L0_conv_qkv_b, L0_conv_proj_w, L0_conv_proj_b, L0_ffn_gate_w, L0_ffn_gate_b, L0_ffn_w_fc, L0_ffn_b_fc, L0_ffn_w_proj, L0_ffn_b_proj, L1_conv_wq, L1_conv_bq, L1_conv_wk, L1_conv_bk, L1_conv_wv, L1_conv_bv, L1_conv_wo, L1_conv_bo, L1_conv_attn_biases, L1_conv_ln1_g, L1_conv_ln1_b, L1_conv_ln3_g, L1_conv_ln3_b, L1_conv_w1, L1_conv_b1, L1_conv_w2, L1_conv_b2, L1_ffn_gate_w, L1_ffn_gate_b, L1_ffn_w1, L1_ffn_b1, L1_ffn_w2, L1_ffn_b2):
    import jax
    import jax.numpy as jnp

    def _L0_conv_ref(x, qkv_w, qkv_b, proj_w, proj_b):
        import jax, jax.numpy as jnp
        import numpy as np
        NUM_HEADS = 12
        B, H, W, C = x.shape
        N = H * W
        nh = NUM_HEADS
        qkv = jnp.einsum('bhwc,dc->bhwd', x, qkv_w) + qkv_b
        qkv = qkv.reshape(B, N, 3, nh, -1)
        q, k, v = (qkv[:, :, 0], qkv[:, :, 1], qkv[:, :, 2])
        q = q.transpose(0, 2, 1, 3)
        k = k.transpose(0, 2, 1, 3)
        v = v.transpose(0, 2, 1, 3)
        hd = q.shape[-1]
        scale = hd ** (-0.5)
        scores = jnp.einsum('bhnd,bhmd->bhnm', q, k) * scale
        attn = jax.nn.softmax(scores.astype(jnp.float32), axis=-1).astype(q.dtype)
        attn = jax.lax.stop_gradient(attn)
        out = jnp.einsum('bhnm,bhmd->bhnd', attn, v)
        out = out.transpose(0, 2, 1, 3).reshape(B, H, W, -1)
        out = jnp.einsum('bhwc,dc->bhwd', out, proj_w) + proj_b
        return out

    def _L0_ffn_ref(x, gate_w, gate_b, w_fc, b_fc, w_proj, b_proj):
        import jax, jax.numpy as jnp
        import numpy as np
        N_EMBD = 384
        HIDDEN = 4 * N_EMBD
        N_EXPERTS = 8
        TOP_K = 2
        B, T, C = x.shape
        E = gate_b.shape[0]
        xf = x.reshape(-1, C)
        scores = xf @ gate_w.T + gate_b
        top_s, top_i = jax.lax.top_k(scores, TOP_K)
        gates = jax.nn.softmax(top_s, axis=-1)
        comb = jnp.sum(jax.nn.one_hot(top_i, E, dtype=xf.dtype) * gates[..., None], axis=1)
        out = jnp.zeros_like(xf)
        for j in range(E):
            h = jax.nn.gelu(xf @ w_fc[j].T + b_fc[j], approximate=True)
            y = h @ w_proj[j].T + b_proj[j]
            out = out + comb[:, j:j + 1] * y
        return out.reshape(B, T, C)

    def _L1_conv_ref(hidden_state, wq, bq, wk, bk, wv, bv, wo, bo, attn_biases, ln1_g, ln1_b, ln3_g, ln3_b, w1, b1, w2, b2):
        import jax, jax.numpy as jnp
        import numpy as np
        D_MODEL = 384
        N_HEADS = 12
        HEAD_DIM = D_MODEL // N_HEADS
        FFN_DIM = 1536
        MAX_WAVELENGTH = 10000.0
        ROPE_PERCENT = 0.5
        NORM_EPS = 1e-05

        def _layernorm(x, g, b):
            mu = jnp.mean(x, axis=-1, keepdims=True)
            var = jnp.mean(jnp.square(x - mu), axis=-1, keepdims=True)
            return (x - mu) * jax.lax.rsqrt(var + NORM_EPS) * g + b

        def _apply_p_rope(x, positions):
            half = HEAD_DIM // 2
            rope_angles = int(ROPE_PERCENT * HEAD_DIM) // 2
            fraction = 2.0 * jnp.arange(rope_angles, dtype=jnp.float32) / HEAD_DIM
            timescale = jnp.concatenate([MAX_WAVELENGTH ** fraction, jnp.full((half - rope_angles,), jnp.inf, dtype=jnp.float32)])
            angles = positions[:, None].astype(jnp.float32) / timescale[None, :]
            sin = jnp.sin(angles)[None, None]
            cos = jnp.cos(angles)[None, None]
            x1, x2 = jnp.split(x, 2, axis=-1)
            return jnp.concatenate([x1 * cos - x2 * sin, x2 * cos + x1 * sin], axis=-1)

        def _forward(hidden_state, wq, bq, wk, bk, wv, bv, wo, bo, attn_biases, ln1_g, ln1_b, ln3_g, ln3_b, w1, b1, w2, b2):
            B, C, S, D = hidden_state.shape
            T = C * S
            flat = hidden_state.reshape(B, T, D)
            ni = _layernorm(flat, ln1_g, ln1_b)
            scaling = HEAD_DIM ** (-0.5)
            q = (ni @ wq + bq) * scaling
            k = ni @ wk + bk
            v = ni @ wv + bv
            to_heads = lambda t: t.reshape(B, T, N_HEADS, HEAD_DIM).transpose(0, 2, 1, 3)
            q, k, v = (to_heads(q), to_heads(k), to_heads(v))
            positions = jnp.arange(T)
            k = _apply_p_rope(k, positions)
            q = _apply_p_rope(q, positions)
            scores = jnp.einsum('bhtd,bhsd->bhts', q, k)
            variate_ids = positions // S
            same = (variate_ids[:, None] == variate_ids[None, :]).astype(scores.dtype)
            variate_bias = same[None, :, :] * attn_biases[:, 0][:, None, None] + (1.0 - same[None, :, :]) * attn_biases[:, 1][:, None, None]
            scores = scores + variate_bias[None]
            probs = jax.nn.softmax(scores, axis=-1)
            attn = jnp.einsum('bhts,bhsd->bhtd', probs, v)
            attn = attn.transpose(0, 2, 1, 3).reshape(B, T, D)
            attn = attn @ wo + bo
            flat = flat + attn
            ff_in = _layernorm(flat, ln3_g, ln3_b)
            ff = jax.nn.gelu(ff_in @ w1 + b1, approximate=False) @ w2 + b2
            flat = flat + ff
            return flat.reshape(B, C, S, D)
        return _forward(hidden_state, wq, bq, wk, bk, wv, bv, wo, bo, attn_biases, ln1_g, ln1_b, ln3_g, ln3_b, w1, b1, w2, b2)

    def _L1_ffn_ref(x, gate_w, gate_b, w1, b1, w2, b2):
        import jax, jax.numpy as jnp
        import numpy as np
        B, S, H, F, E = (8, 256, 384, 1536, 6)
        TOP_K = 2
        b, s, h = x.shape
        xf = x.reshape(-1, h)
        gate_scores = xf @ gate_w + gate_b
        topk_scores, topk_idx = jax.lax.top_k(gate_scores, TOP_K)
        topk_weights = jax.nn.softmax(topk_scores, axis=1)
        hmid = jax.nn.gelu(jnp.einsum('nh,ehf->nef', xf, w1) + b1, approximate=False)
        expert_out = jnp.einsum('nef,efh->neh', hmid, w2) + b2
        sel = jnp.take_along_axis(expert_out, topk_idx[:, :, None], axis=1)
        out = jnp.einsum('nk,nkh->nh', topk_weights, sel)
        return out.reshape(b, s, h)

    def _gn(v, G=32, eps=1e-05):
        B_, H_, W_, C_ = v.shape
        g = v.reshape(B_, H_, W_, G, C_ // G)
        m = jnp.mean(g, axis=(1, 2, 4), keepdims=True)
        s = jnp.var(g, axis=(1, 2, 4), keepdims=True)
        return ((g - m) / jnp.sqrt(s + eps)).reshape(v.shape)

    def _ln_c(v, eps=1e-06):
        m = jnp.mean(v, axis=-1, keepdims=True)
        s = jnp.var(v, axis=-1, keepdims=True)
        return (v - m) / jnp.sqrt(s + eps)

    def _ln_t(v, eps=1e-05):
        m = jnp.mean(v, axis=-1, keepdims=True)
        s = jnp.var(v, axis=-1, keepdims=True)
        return (v - m) / jnp.sqrt(s + eps)

    def _to_tokens(v):
        B_, H_, W_, C_ = v.shape
        return v.reshape(B_, H_ * W_, C_)

    def _from_tokens(t, like):
        return t.reshape(like.shape)
    x = x + _L0_conv_ref(_ln_c(x), L0_conv_qkv_w, L0_conv_qkv_b, L0_conv_proj_w, L0_conv_proj_b)
    t = _to_tokens(x)
    t = t + _L0_ffn_ref(_ln_t(t), L0_ffn_gate_w, L0_ffn_gate_b, L0_ffn_w_fc, L0_ffn_b_fc, L0_ffn_w_proj, L0_ffn_b_proj)
    x = _from_tokens(t, x)
    x = x + _L1_conv_ref(_ln_c(x), L1_conv_wq, L1_conv_bq, L1_conv_wk, L1_conv_bk, L1_conv_wv, L1_conv_bv, L1_conv_wo, L1_conv_bo, L1_conv_attn_biases, L1_conv_ln1_g, L1_conv_ln1_b, L1_conv_ln3_g, L1_conv_ln3_b, L1_conv_w1, L1_conv_b1, L1_conv_w2, L1_conv_b2)
    t = _to_tokens(x)
    t = t + _L1_ffn_ref(_ln_t(t), L1_ffn_gate_w, L1_ffn_gate_b, L1_ffn_w1, L1_ffn_b1, L1_ffn_w2, L1_ffn_b2)
    x = _from_tokens(t, x)
    return x

_drawn_inputs = setup_inputs


def setup_inputs(seed=0):
    import zlib

    import numpy as np

    out = dict(_drawn_inputs(seed))
    spreads = {'L0_conv_qkv_b': (0.0, 0.1),
     'L0_conv_proj_b': (0.0, 0.1),
     'L0_ffn_gate_b': (0.0, 0.1),
     'L0_ffn_b_fc': (0.0, 0.1),
     'L0_ffn_b_proj': (0.0, 0.1),
     'L1_conv_bq': (0.0, 0.8),
     'L1_conv_bk': (0.0, 0.8),
     'L1_conv_bv': (0.0, 0.374),
     'L1_conv_bo': (0.0, 0.1),
     'L1_conv_ln1_g': (1.0, 0.6),
     'L1_conv_ln1_b': (0.0, 0.529),
     'L1_conv_ln3_g': (1.0, 0.6),
     'L1_conv_ln3_b': (0.0, 0.564),
     'L1_conv_b1': (0.0, 0.276),
     'L1_conv_b2': (0.0, 0.1)}
    factors = {'L1_conv_wq': 8.0,
     'L1_conv_wk': 8.0,
     'L1_conv_attn_biases': 64.0,
     'L1_ffn_gate_b': 4.014,
     'L1_ffn_b1': 24.441,
     'L1_ffn_b2': 8.0}
    for name, (base, spread) in spreads.items():
        noise = np.random.default_rng([zlib.crc32(name.encode()), seed]).standard_normal(out[name].shape)
        drawn = base * np.exp(spread * noise) if base else spread * noise
        out[name] = jnp.asarray(drawn.astype(out[name].dtype))
    for name, factor in factors.items():
        out[name] = (out[name] * factor).astype(out[name].dtype)
    return out
```

```python
from contextlib import ExitStack

import numpy as np
import concourse.bass as bass
from concourse import mybir

F32 = mybir.dt.float32
F32R = mybir.dt.float32r
BF16 = mybir.dt.bfloat16
U32 = mybir.dt.uint32
ALU = mybir.AluOpType
ACT = mybir.ActivationFunctionType
AX = mybir.AxisListType

P = 128
T = 1024
C = 384
F = 1536
NT = T // P
NC_ = C // P
NF = F // P
H = 12
D = C // H
HPC = P // D
SCALE = float(D) ** -0.5
HALF = 512
NH = T // HALF
S = 32
V = P // S
ROPE = 8
E0, E1 = 8, 6
EM = 8
TOP = 2
TILES = (TOP * T + (P - 1) * EM) // P
CLEARED = TILES + 2
SLOTS = (TILES + EM + 1) * P
QUARTER = 256
NQ = T // QUARTER
ROW_MAX = 96
P_RING = 3
LEAD = 14
NEG = 2


def build(nc, a, out):
    with ExitStack() as ctx:
        program(nc, a, out, ctx)


def maxima_order():
    order = []
    for h in range(H):
        for t in range(NT):
            order.append(("tile", h, t))
            if h and t == NEG - 1:
                order.append(("turn", h - 1, 0))
    order.append(("turn", H - 1, 0))
    return order


def program(nc, a, out, ctx):
    def sb(name, shape, dt=F32, where=ctx):
        return where.enter_context(nc.sbuf_tensor(name, shape, dt))

    def sem(name):
        return ctx.enter_context(nc.semaphore(name))

    grouped = nc.dram_tensor("grouped", (SLOTS, C), F32, kind="Internal").ap()
    expert_out = nc.dram_tensor("expert_out", (SLOTS, C), F32, kind="Internal").ap()

    LN_PE = {0: 0, 1: NT, 3: 2 * NT, 4: 3 * NT, 5: 4 * NT}
    XN = {k: NT * k for k in range(6)}

    x_res = sb("x_res", [P, NT, C])
    flat = sb("flat", [P, NT, C])
    xT = sb("xT", [P, NC_, T])
    xn = sb("xn", [P, 2, C])
    ident = sb("ident", [P, P])
    bn_raw = sb("bn_raw", [P, NT, 6])
    bn_mv = sb("bn_mv", [P, NT, 2])
    var_eps = sb("var_eps", [P, NT])
    std = sb("std", [P, NT])
    rstd0 = sb("rstd0", [P, NT])
    newton = sb("newton", [P, NT])
    rstd = sb("rstd", [P, NT])
    affine = sb("affine", [P, 2, 2, NC_])
    attT = xT

    with ExitStack() as att:
        q_stack = sb("q_stack", [P, H, T], F32R, att)
        k_stack = sb("k_stack", [P, H, T], F32R, att)
        v_tok = sb("v_tok", [P, NT, C], F32, att)
        w_qkv = sb("w_qkv", [P, NC_, 3 * C], F32, att)
        w_o = sb("w_o", [P, NC_, C], F32, att)
        b_qkv = sb("b_qkv", [P, 3 * C], F32, att)
        b_o = sb("b_o", [P, C], F32, att)
        ones_v = sb("ones_v", [P, D], F32, att)
        neg_max = sb("neg_max", [P, H, NT], F32, att)
        row_max = sb("row_max", [P, H, NT], F32, att)
        variate = sb("variate", [P, 12, H], F32, att)
        key_of = sb("key_of", [P, P], BF16, att)
        bias_of = sb("bias_of", [P, H, P], BF16, att)
        trig = sb("trig", [P, 2, NT, ROPE], F32, att)
        shift = sb("shift", [NT, 2, P], F32R, att)
        with ExitStack() as early:
            stage = sb("stage", [P, 2, 4, NC_, QUARTER], F32R, early)
            qk_tok = sb("qk_tok", [P, 2 * C], F32, early)
            rot = sb("rot", [P, 4, H, ROPE], F32, early)
        probs = sb("probs", [P, P_RING, T], F32, att)
        rden = sb("rden", [D, NH, HALF], F32, att)

    with ExitStack() as ff:
        w1 = [sb(f"w1_{i}", [P, NC_, F], F32, ff) for i in range(2)]
        w2 = [sb(f"w2_{i}", [P, NF, C], F32, ff) for i in range(2)]
        hT = sb("hT", [P, 2, NF, HALF], F32, ff)
        x_tile = sb("x_tile", [P, C], F32, ff)
        xT_tile = sb("xT_tile", [P, NC_, P], F32, ff)
        y_tile = sb("y_tile", [P, C], F32, ff)
        y_got = sb("y_got", [P, TOP, NT, C], F32, ff)
        tri = sb("tri", [P, P], F32, ff)
        ones = sb("ones", [P, P], F32, ff)
        limits = sb("limits", [P, EM - 1], F32, ff)
        pick = sb("pick", [P, TOP, NT, EM], F32, ff)
        routed = sb("routed", [P, NT, EM], F32, ff)
        total = sb("total", [P, EM, NT], F32, ff)
        upto = sb("upto", [P, EM, NT], F32, ff)
        before = sb("before", [P, EM, NT], F32, ff)
        count = sb("count", [P, EM], F32, ff)
        filled = sb("filled", [P, EM, EM - 1], F32, ff)
        tiles = sb("tiles", [P, 2, EM], F32, ff)
        tiles_upto = sb("tiles_upto", [P, EM], F32, ff)
        offset = sb("offset", [P, EM], F32, ff)
        place = sb("place", [P, NT, EM], F32, ff)
        picked = sb("picked", [P, TOP, NT, EM], F32, ff)
        slot_f = sb("slot_f", [P, TOP, NT], F32, ff)
        slot = sb("slot", [P, TOP, NT], U32, ff)
        plan = sb("plan", [1, 2, EM], mybir.dt.int32, ff)
        b1 = sb("b1", [P, 15, NF], F32, ff)
        b2 = sb("b2", [8, C], F32, ff)
        w_gate = sb("w_gate", [P, NC_, 8], F32, ff)
        b_gate = sb("b_gate", [P, 8], F32, ff)
        scores = sb("scores", [P, NT, 8], F32, ff)
        top = sb("top", [P, NT, 8], F32, ff)
        top_i = sb("top_i", [P, NT, 8], U32, ff)
        top_f = sb("top_f", [P, NT, 2], F32, ff)
        lanes = sb("lanes", [P, 8], F32, ff)
        gates = sb("gates", [P, 4, NT], F32, ff)
        comb = sb("comb", [P, NT, 8], F32, ff)
        comb2 = sb("comb2", [P, NT, 8], F32, ff)
        combT = sb("combT", [8, T], F32, ff)
        ones_row = ones[0:1, :]

    bank = ctx.enter_context(nc.psum_tensor("bank", [P, 8, HALF], F32))

    G = {}

    def named(name):
        if name not in G:
            G[name] = sem(name)
        return G[name]

    loads = {}

    block = ctx.enter_context(nc.Block())

    @block.sync
    def _(sp):
        def load(name, dst, src):
            sp.dma_start(dst, src).then_inc(named(name), 16)
            loads[name] = loads.get(name, 0) + 16

        def attention_weights(n, pre):
            load(f"{pre}w", w_qkv[:, :, :], a[f"{pre}qkv"].rearrange("(c p) n -> p c n", p=P))
            load(f"{pre}w", b_qkv[:, :], a[f"{pre}bqkv"].partition_broadcast(P))
            load(f"{pre}w2", w_o[:, :, :], a[f"{pre}wo"].rearrange("(c p) n -> p c n", p=P))
            load(f"{pre}w2", b_o[:, :], a[f"{pre}bo"].partition_broadcast(P))

        def stacks(n, pre):
            for qr in range(NQ):
                done = named(f"{pre}stack{qr % 2}")
                sp.wait_ge(named(f"{pre}lo"), 2 * (qr + 1))
                tok = slice(qr * QUARTER, (qr + 1) * QUARTER)
                for j in range(HPC):
                    for stack, rows, kind in ((q_stack, 0, 0), (q_stack, 1, 1), (q_stack, 2, 0),
                                              (k_stack, 0, 2), (k_stack, 1, 2), (k_stack, 2, 3)):
                        sp.dma_start(stack[D * rows:D * rows + D, j:H:HPC, tok].bitcast(F32),
                                     stage[D * j:D * j + D, qr % 2, kind, :, :].bitcast(F32)).then_inc(done, 16)
            for h in range(H):
                sp.wait_ge(named(f"{pre}shift"), h + 1)
                sp.dma_start(q_stack[ROW_MAX:ROW_MAX + 1, h, :].rearrange("p (t q) -> p t q", t=NT).bitcast(F32),
                             shift[:, h % 2, :].bitcast(F32)).then_inc(named(f"{pre}shifted{h % 2}"), 16)

        def weights(name, at, w1_src, w2_src):
            sp.dma_start(w1[at][:, :, :], w1_src.rearrange("(c p) n -> p c n", p=P)).then_inc(named(name), 16)
            sp.dma_start(w2[at][:, :, :], w2_src.rearrange("(c p) n -> p c n", p=P)).then_inc(named(name), 16)

        def later_experts(pre, n_e, flip):
            src1 = a[f"{pre}w1"].rearrange("e k n -> (e k) n")
            src2 = a[f"{pre}w2"].rearrange("e k n -> (e k) n")
            sp.wait_ge(named("plan"), 1 + (pre == "l1"))
            with sp.Fori(1, n_e // 2) as pair:
                for s in range(2):
                    e = pair * 2 + s
                    through = sp.value_load(plan[0:1, 1, bass.ds(e - 1, 1)], min_val=1, max_val=TILES)
                    rows1 = src1[bass.ds(e * C, C), :]
                    rows2 = src2[bass.ds(e * F, F), :]
                    sp.wait_ge(named(f"{pre}y_mm"), through)
                    weights(f"{pre}w{s}_", s ^ flip, rows1, rows2)

        for half in range(2):
            load("x_in", x_res[:, 4 * half:4 * half + 4, :],
                 a["x"][half * HALF:half * HALF + HALF, :].rearrange("(t p) c -> p t c", p=P))
        load("const", affine[:, :, :, :], a["affine"])
        attention_weights(0, "l0")
        stacks(0, "l0")
        sp.wait_ge(named("l0proj_add"), NT)
        load("ffc", b1[:, :, :], a["b1"])
        load("ffc", b2[:, :], a["l0b2"])
        load("ffc", w_gate[:, :, :], a["l0gate_w"].rearrange("(c p) n -> p c n", p=P))
        load("ffc", b_gate[:, :], a["l0gate_b"].partition_broadcast(P))
        for s in range(2):
            weights(f"l0w{s}_", s, a["l0w1"][s], a["l0w2"][s])
        later_experts("l0", E0, 0)
        sp.wait_ge(named("l0mix"), NT)
        attention_weights(1, "l1")
        load("l1trig", trig[:, :, :, :], a["trig"])
        load("l1bias", variate[:, 0:2, :], a["attn_biases"].partition_broadcast(P))
        stacks(1, "l1")
        sp.wait_ge(named("l1proj_add"), NT)
        load("ffc", b1[:, :, :], a["b1"])
        load("ffc", b2[0:1, :], a["mlp_b2"])
        weights("mlpw", 0, a["mlp_w1"], a["mlp_w2"])
        weights("l1w0_", 1, a["l1w1"][0], a["l1w2"][0])
        sp.wait_ge(named("ff_add"), NT)
        load("ffc", b2[0:E1, :], a["l1b2"])
        load("ffc", w_gate[:, :, 0:E1], a["l1gate_w"].rearrange("(c p) n -> p c n", p=P))
        load("ffc", b_gate[:, 0:E1], a["l1gate_b"].partition_broadcast(P))
        weights("l1w1_", 0, a["l1w1"][1], a["l1w2"][1])
        later_experts("l1", E1, 1)
        for t in range(NT):
            sp.wait_ge(named("l1mix"), t + 1)
            sp.dma_start(out[t * P:(t + 1) * P, :], x_res[:, t, :]).then_inc(named("stored"), 16)
        sp.wait_ge(named("stored"), 16 * NT)

    FFC = [64, 96, 144]

    def variate_tables(pool):
        done = named("vt")
        n = [0]

        def step(ins):
            n[0] += 1
            ins.then_inc(done, 1)
            pool.wait_ge(done, n[0])

        pool.wait_ge(named("l1bias"), 16)
        diff, p1, p2, p3 = (variate[:, i, :] for i in (2, 3, 4, 5))
        r1, r2 = (variate[:, i, :] for i in (6, 7))
        step(pool.tensor_tensor(diff, variate[:, 0, :], variate[:, 1, :], ALU.subtract))
        step(pool.tensor_scalar(diff, diff, float(D) ** 0.5, 0.0, ALU.mult, ALU.add))
        pieces = bias_of[:, 0, 0:3 * H].rearrange("p (i h) -> p i h", i=3)
        step(pool.tensor_copy(pieces[:, 0, :], diff))
        step(pool.tensor_copy(p1, pieces[:, 0, :]))
        step(pool.tensor_tensor(r1, diff, p1, ALU.subtract))
        step(pool.tensor_copy(pieces[:, 1, :], r1))
        step(pool.tensor_copy(p2, pieces[:, 1, :]))
        step(pool.tensor_tensor(r2, r1, p2, ALU.subtract))
        step(pool.tensor_copy(pieces[:, 2, :], r2))
        step(pool.tensor_copy(p3, pieces[:, 2, :]))
        own = variate[:, 8, :]
        for i, piece in ((9, p1), (10, p2), (11, p3)):
            lo = V * (i - 9)
            step(pool.affine_select(out=variate[:, i, :], in_=piece, compare_op=ALU.is_ge, fill=0.0, base=-lo,
                                    pattern=[[0, H]], channel_multiplier=1))
            step(pool.affine_select(out=variate[:, i, :], in_=variate[:, i, :], compare_op=ALU.is_ge, fill=0.0,
                                    base=lo + V - 1, pattern=[[0, H]], channel_multiplier=-1))
        step(pool.tensor_tensor(own, variate[:, 9, :], variate[:, 10, :], ALU.add))
        step(pool.tensor_tensor(own, own, variate[:, 11, :], ALU.add))
        step(pool.memset(key_of[:, :], 0.0))
        for i in range(3):
            for v in range(V):
                step(pool.affine_select(out=key_of[:, S * v:S * v + S], in_=key_of[:, S * v:S * v + S],
                                        compare_op=ALU.not_equal, fill=1.0, base=-(V * i + v),
                                        pattern=[[0, S]], channel_multiplier=1))
        for h in range(H):
            pool.tensor_scalar(bias_of[:, h, :], key_of[:, :], own[:, h:h + 1], None,
                               ALU.mult).then_inc(named("bias_of"), 1)

    def tables(pool, n):
        done = named("tables")
        pool.memset(tri[:, :], 0.0).then_inc(done, 1)
        pool.wait_ge(done, 6 * n + 1)
        pool.affine_select(out=tri[:, :], in_=tri[:, :], compare_op=ALU.is_ge, fill=1.0, base=0,
                           pattern=[[-1, P]], channel_multiplier=1).then_inc(done, 1)
        pool.wait_ge(done, 6 * n + 2)
        pool.memset(ones[:, :], 1.0).then_inc(done, 1)
        pool.wait_ge(done, 6 * n + 3)
        pool.iota(lanes[:, :], pattern=[[1, EM]], base=0, channel_multiplier=0,
                  allow_small_or_imprecise_dtypes=True).then_inc(done, 1)
        pool.wait_ge(done, 6 * n + 4)
        pool.iota(limits[:, :], pattern=[[P, EM - 1]], base=P, channel_multiplier=0,
                  allow_small_or_imprecise_dtypes=True).then_inc(done, 1)
        pool.wait_ge(done, 6 * n + 5)
        pool.memset(y_tile[:, :], 0.0).then_inc(done, 1)
        pool.wait_ge(done, 6 * n + 6)

    def exchange(pool, n, pre, n_e):
        if not n:
            pool.wait_ge(named("cleared"), 32)
        pool.wait_ge(named("slots"), n + 1)
        for t in range(NT):
            for j in range(TOP):
                pool.indirect_dma_start(grouped[:, :], bass.IndirectOffsetOnAxis(ap=slot[:, j, t:t + 1], axis=0),
                                        flat[:, t, :], None).then_inc(named(f"{pre}sent"), 16)
        pool.wait_ge(named(f"{pre}sent"), 16 * TOP * NT)
        loaded, turned, out_free = named(f"{pre}x_in"), named(f"{pre}x_tr"), named(f"{pre}y_sb")
        pool.dma_start(x_tile[:, :], grouped[0:P, :]).then_inc(loaded, 16)
        pool.dma_start(expert_out[0:P, :], y_tile[:, :]).then_inc(named(f"{pre}y_out"), 16)
        pool.wait_ge(turned, 1)
        pool.dma_start(x_tile[:, :], grouped[P:2 * P, :]).then_inc(loaded, 16)
        with pool.Fori(0, n_e) as e:
            n_tiles = pool.value_load(plan[0:1, 0, bass.ds(e, 1)], min_val=1, max_val=EM)
            first = pool.value_load(plan[0:1, 1, bass.ds(e, 1)], min_val=0, max_val=TILES - 1)
            with pool.Fori(0, n_tiles) as i:
                g = first + i
                src = grouped[bass.ds(g * P + 2 * P, P), :]
                dst = expert_out[bass.ds(g * P, P), :]
                pool.wait_ge(turned, g + 2)
                pool.dma_start(x_tile[:, :], src).then_inc(loaded, 16)
                pool.wait_ge(out_free, g + 2)
                pool.dma_start(dst, y_tile[:, :]).then_inc(named(f"{pre}y_out"), 16)
        pool.wait_ge(named("all_out"), n + 1)
        for t in range(NT):
            for j in range(TOP):
                pool.indirect_dma_start(y_got[:, j, t, :], None, expert_out[0:CLEARED * P, :],
                                        bass.IndirectOffsetOnAxis(ap=slot[:, j, t:t + 1], axis=0)
                                        ).then_inc(named(f"{pre}got"), 16)

    @block.gpsimd
    def _(pool):
        pool.memset(ident[:, :], 0.0).then_inc(named("id0"), 1)
        pool.wait_ge(named("id0"), 1)
        pool.affine_select(out=ident[:, :], in_=ident[:, :], compare_op=ALU.not_equal, fill=1.0, base=0,
                           pattern=[[-1, P]], channel_multiplier=1).then_inc(named("ident"), 1)
        pool.wait_ge(named("ident"), 1)
        pool.memset(xn[:, 0, :], 0.0).then_inc(named("zeros"), 1)
        pool.wait_ge(named("zeros"), 1)
        for scratch in (grouped, expert_out):
            pool.dma_start(scratch[0:CLEARED * P, :].rearrange("(t p) c -> p t c", p=P),
                           xn[:, 0, :].unsqueeze(1).to_broadcast([P, CLEARED, C])).then_inc(named("cleared"), 16)
        for n, pre in enumerate(("l0", "l1")):
            if n:
                pool.wait_ge(named("l0mix"), NT)
            pool.memset(k_stack[ROW_MAX:ROW_MAX + 1, :, :].bitcast(F32), 1.0).then_inc(named("ones"), 1)
            pool.wait_ge(named("ones"), 2 * n + 1)
            pool.memset(ones_v[:, :], 1.0).then_inc(named("ones"), 1)
            if n:
                variate_tables(pool)
            pool.wait_ge(named("ones"), 2 * n + 2)
            acc = flat if n else x_res
            pool.wait_ge(named(f"{pre}w2"), 32)
            pool.wait_ge(named("xn"), NT * (4 if n else 1))
            for t in range(NT):
                pool.tensor_tensor(acc[:, t, :], acc[:, t, :], b_o[:, :], ALU.add).then_inc(named(f"{pre}bo"), 1)
            pool.wait_ge(named(f"{pre}proj_add"), NT)
            tables(pool, n)
            exchange(pool, n, pre, E1 if n else E0)

    @block.vector
    def _(dve):
        chain = [0]

        def step(ins):
            chain[0] += 1
            ins.then_inc(named("dve_chain"), 1)
            dve.wait_ge(named("dve_chain"), chain[0])

        def stats(src, t):
            step(dve.bn_stats(bn_raw[:, t, :], src[:, t, :]))
            dve.bn_aggr(bn_mv[:, t, :], bn_raw[:, t, :]).then_inc(named("stats"), 1)

        def normalize(k, src, eps, dst=None):
            dve.wait_ge(named("stats"), NT * (k + 1))
            dve.tensor_scalar(var_eps[:, :], bn_mv[:, :, 1], eps, None, ALU.add).then_inc(named("var"), 1)
            dve.wait_ge(named("std"), k + 1)
            step(dve.reciprocal(rstd0[:, :], std[:, :]))
            step(dve.tensor_tensor(newton[:, :], rstd0[:, :], rstd0[:, :], ALU.mult))
            step(dve.tensor_tensor(newton[:, :], newton[:, :], var_eps[:, :], ALU.mult))
            step(dve.tensor_scalar(newton[:, :], newton[:, :], -0.5, 1.5, ALU.mult, ALU.add))
            step(dve.tensor_tensor(rstd[:, :], newton[:, :], rstd0[:, :], ALU.mult))
            for t in range(NT):
                if dst is None:
                    if t >= 2:
                        dve.wait_ge(named("ln_tr"), LN_PE[k] + t - 1)
                    elif k == 0:
                        dve.wait_ge(named("cleared"), 32)
                to = dst[:, t, :] if dst is not None else xn[:, t % 2, :]
                dve.tensor_scalar(to, src[:, t, :], bn_mv[:, t, 0:1], rstd[:, t:t + 1],
                                  ALU.subtract, ALU.mult).then_inc(named("xn"), 1)

        def qkv(n, pre):
            dve.wait_ge(named(f"{pre}w"), 32)
            if n:
                dve.wait_ge(named("l1trig"), 16)
            for t in range(NT + 1):
                if t < NT:
                    b = 3 * (t % 2)
                    dve.wait_ge(named(f"{pre}qkv_mm"), t + 1)
                    if t:
                        dve.wait_ge(named(f"{pre}qk_tr"), t)
                    for i in range(2):
                        ins = dve.tensor_tensor(qk_tok[:, C * i:C * i + C], bank[:, b + i, 0:C],
                                                b_qkv[:, C * i:C * i + C], ALU.add)
                    if n:
                        step(ins)
                        ins = rope(t)
                    ins.then_inc(named(f"{pre}qk"), 1)
                    dve.tensor_tensor(v_tok[:, t, :], bank[:, b + 2, 0:C], b_qkv[:, 2 * C:3 * C],
                                      ALU.add).then_inc(named(f"{pre}v"), 1)
                if t:
                    u = t - 1
                    dve.wait_ge(named(f"{pre}hi"), u + 1)
                    if u % 2 == 0 and u >= 4:
                        dve.wait_ge(named(f"{pre}stack{u // 2 % 2}"), 16 * 24 * (u // 4))
                    for i in range(2):
                        tok = slice(P * (u % 2), P * (u % 2) + P)
                        ins = dve.tensor_tensor(stage[:, u // 2 % 2, 2 * i + 1, :, tok],
                                                bank[:, 6 + i, 0:C].rearrange("p (c q) -> p c q", c=NC_),
                                                stage[:, u // 2 % 2, 2 * i, :, tok].bitcast(F32), ALU.subtract)
                    ins.then_inc(named(f"{pre}lo"), 1)

        def rope(t):
            cos = trig[:, 0, t, :].unsqueeze(1).to_broadcast([P, H, ROPE])
            sin = trig[:, 1, t, :].unsqueeze(1).to_broadcast([P, H, ROPE])
            for i in range(2):
                qk = qk_tok[:, C * i:C * i + C].rearrange("p (h d) -> p h d", h=H)
                x1, x2 = qk[:, :, 0:ROPE], qk[:, :, D // 2:D // 2 + ROPE]
                dve.tensor_tensor(rot[:, 0], x1, cos, ALU.mult)
                dve.tensor_tensor(rot[:, 1], x2, sin, ALU.mult)
                dve.tensor_tensor(rot[:, 2], x2, cos, ALU.mult)
                step(dve.tensor_tensor(rot[:, 3], x1, sin, ALU.mult))
                dve.tensor_tensor(x1, rot[:, 0], rot[:, 1], ALU.subtract)
                ins = dve.tensor_tensor(x2, rot[:, 2], rot[:, 3], ALU.add)
                if i == 0:
                    step(ins)
            return ins

        def attention(n, pre):
            order = maxima_order()
            at = [0]

            def maxima(count):
                for _ in range(count):
                    if at[0] == len(order):
                        return
                    kind, h, t = order[at[0]]
                    dve.wait_ge(named(f"{pre}mx_mm"), at[0] + 1)
                    pair = 2 * (at[0] % 2)
                    if kind == "tile":
                        ins = dve.tensor_reduce(row_max[:, h, t:t + 1], bank[:, pair:pair + 2, :], AX.XY, ALU.max)
                        ins.then_inc(named(f"{pre}mx_read"), 1)
                        if t == NT - 1:
                            dve.wait_ge(named(f"{pre}mx_read"), NT * (h + 1))
                            dve.tensor_scalar(neg_max[:, h, :], row_max[:, h, :], -1.0, None,
                                              ALU.mult).then_inc(named(f"{pre}neg"), 1)
                    else:
                        if h >= 2:
                            dve.wait_ge(named(f"{pre}shifted{h % 2}"), 16 * (h // 2))
                        dve.tensor_copy(shift[:, h % 2, :], bank[0:NT, pair, 0:P]).then_inc(named(f"{pre}shift"), 1)
                    at[0] += 1

            def finish(h):
                dve.wait_ge(named(f"{pre}pv"), NT * (h + 1))
                j, c = h % HPC, h // HPC
                for half in range(NH):
                    b = 6 + (h + half) % 2
                    acc = bank[64 * half:64 * half + D, b, :]
                    den = bank[64 * half + D:64 * half + 2 * D, b, :]
                    r = rden[:, half, :]
                    step(dve.reciprocal(r, den))
                    ins = dve.tensor_tensor(attT[D * j:D * j + D, c, half * HALF:half * HALF + HALF], acc, r, ALU.mult)
                    ins.then_inc(named(f"{pre}att"), 1)

            maxima(LEAD)
            for h in range(H):
                for kt in range(NT):
                    maxima(1 + (kt == 0))
                    if kt == 2 and h:
                        finish(h - 1)
            maxima(len(order))
            finish(H - 1)

        def project(n, pre, acc):
            for t in range(NT):
                dve.wait_ge(named(f"{pre}proj"), t + 1)
                dve.wait_ge(named(f"{pre}bo"), NT)
                dve.tensor_tensor(acc[:, t, :], acc[:, t, :], bank[:, t % 4, 0:C],
                                  ALU.add).then_inc(named(f"{pre}proj_add"), 1)
                dve.wait_ge(named(f"{pre}proj_add"), t + 1)
                if n:
                    step(dve.tensor_tensor(x_res[:, t, :], x_res[:, t, :], acc[:, t, :], ALU.add))
                stats(acc, t)

        def gating(k, n_e, ffc):
            dve.wait_ge(named("ffc"), ffc)
            dve.wait_ge(named("tables"), 6 * (k + 1))
            if n_e < EM:
                step(dve.memset(scores[:, :, n_e:EM], -3.0e38))
            for t in range(NT):
                dve.wait_ge(named("gate_mm"), NT * k + t + 1)
                step(dve.tensor_tensor(scores[:, t, 0:n_e], bank[:, 4 + t % 2, 0:n_e], b_gate[:, 0:n_e], ALU.add))
                step(dve.max(top[:, t, :], scores[:, t, :]))
                dve.max_index(top_i[:, t, :], top[:, t, :], scores[:, t, :]).then_inc(named("gate_top"), 1)
            dve.wait_ge(named("gate_top"), NT * (k + 1))
            dve.tensor_tensor(gates[:, 0, :], top[:, :, 1], top[:, :, 0], ALU.subtract).then_inc(named("gap"), 1)
            step(dve.tensor_copy(top_f[:, :, :], top_i[:, :, 0:TOP]))

        def routing(k, n_e):
            wide = [P, NT, EM]
            for j in range(TOP):
                ins = dve.tensor_tensor(pick[:, j], lanes[:, :].unsqueeze(1).to_broadcast(wide),
                                        top_f[:, :, j].unsqueeze(2).to_broadcast(wide), ALU.is_equal)
            step(ins)
            dve.tensor_tensor(routed[:, :, :], pick[:, 0], pick[:, 1], ALU.add).then_inc(named("routed"), 1)
            dve.wait_ge(named("counted"), k + 1)
            step(dve.tensor_copy(total[:, :, :], bank[:, 5, 0:NT * EM].rearrange("p (t e) -> p e t", t=NT)))
            flat_et = lambda x: x[:, :, :].rearrange("p e t -> p (e t)")
            step(dve.tensor_tensor_scan(flat_et(upto), ones[:, 0:EM * NT], flat_et(total), 0.0, ALU.mult, ALU.add))
            step(dve.tensor_tensor(before[:, :, :], upto[:, :, :], total[:, :, :], ALU.subtract))
            step(dve.tensor_tensor(count[:, :], upto[:, :, NT - 1], before[:, :, 0], ALU.subtract))
            step(dve.tensor_tensor(filled[:, :, :], count[:, :].unsqueeze(2).to_broadcast([P, EM, EM - 1]),
                                   limits[:, :].unsqueeze(1).to_broadcast([P, EM, EM - 1]), ALU.is_gt))
            step(dve.tensor_reduce(tiles[:, 0, :], filled[:, :, :], AX.X, ALU.add))
            step(dve.tensor_scalar(tiles[:, 0, :], tiles[:, 0, :], 1.0, None, ALU.add))
            step(dve.tensor_tensor_scan(tiles_upto[:, :], ones[:, 0:EM], tiles[:, 0, :], 0.0, ALU.mult, ALU.add))
            step(dve.tensor_tensor(tiles[:, 1, :], tiles_upto[:, :], tiles[:, 0, :], ALU.subtract))
            dve.tensor_copy(plan[:, :, :], tiles[0:1, :, :]).then_inc(named("plan"), 1)
            step(dve.scalar_tensor_tensor(out=offset[:, :], in0=tiles[:, 1, :], scalar=float(P),
                                          in1=before[:, :, 0], op0=ALU.mult, op1=ALU.subtract))
            step(dve.tensor_tensor(place[:, :, :], before[:, :, :].rearrange("p e t -> p t e"),
                                   bank[:, 4, 0:NT * EM].rearrange("p (t e) -> p t e", t=NT), ALU.add))
            step(dve.tensor_tensor(place[:, :, :], place[:, :, :], offset[:, :].unsqueeze(1).to_broadcast(wide),
                                   ALU.add))
            for j in range(TOP):
                ins = dve.tensor_tensor(picked[:, j], pick[:, j], place[:, :, :], ALU.mult)
            step(ins)
            step(dve.tensor_reduce(slot_f[:, :, :], picked[:, :, :, :], AX.X, ALU.add))
            dve.tensor_copy(slot[:, :, :], slot_f[:, :, :]).then_inc(named("slots"), 1)

        def output_bias(k):
            dve.wait_ge(named("gap_exp"), k + 1)
            step(dve.tensor_scalar(gates[:, 2, :], gates[:, 1, :], 1.0, None, ALU.add))
            step(dve.reciprocal(gates[:, 3, :], gates[:, 2, :]))
            step(dve.tensor_tensor(gates[:, 2, :], gates[:, 1, :], gates[:, 3, :], ALU.mult))
            for j, gate in ((0, 3), (1, 2)):
                to = comb if j else comb2
                step(dve.tensor_tensor(to[:, :, :], pick[:, j],
                                       gates[:, gate, :].unsqueeze(2).to_broadcast([P, NT, EM]), ALU.mult))
            dve.tensor_tensor(comb[:, :, :], comb[:, :, :], comb2[:, :, :], ALU.add).then_inc(named("comb"), 1)
            for t in range(NT):
                dve.wait_ge(named("comb_tr"), NT * k + t + 1)
                dve.tensor_copy(combT[:, t * P:(t + 1) * P], bank[0:EM, 4 + t % 2, 0:P]).then_inc(named("combT"), 1)
            for t in range(NT):
                dve.wait_ge(named("b2_mm"), NT * k + t + 1)
                dve.tensor_tensor(x_res[:, t, :], x_res[:, t, :], bank[:, 6 + t % 2, 0:C],
                                  ALU.add).then_inc(named("b2_add"), 1)
            dve.wait_ge(named("b2_add"), NT * (k + 1))

        def experts(k, pre, n_e):
            y_sb, y_out = named(f"{pre}y_sb"), named(f"{pre}y_out")
            dve.tensor_copy(count[:, 0:1], tiles_upto[:, 0:1]).then_inc(y_sb, 1)

            def rows_in():
                return dve.tensor_copy(xT_tile[:, :, :], bank[:, 6, 0:C].rearrange("p (c q) -> p c q", c=NC_))

            dve.wait_ge(named(f"{pre}x_tr"), 1)
            rows_in().then_inc(named(f"{pre}xT_sb"), 1)
            dve.wait_ge(named("plan"), k + 1)
            with dve.Fori(0, n_e) as e:
                n_tiles = dve.value_load(plan[0:1, 0, bass.ds(e, 1)], min_val=1, max_val=EM)
                first = dve.value_load(plan[0:1, 1, bass.ds(e, 1)], min_val=0, max_val=TILES - 1)
                with dve.Fori(0, n_tiles) as i:
                    g = first + i
                    dve.wait_ge(named(f"{pre}x_tr"), g + 2)
                    rows_in().then_inc(named(f"{pre}xT_sb"), 1)
                    dve.wait_ge(named(f"{pre}y_mm"), g + 1)
                    dve.wait_ge(y_out, g * 16 + 16)
                    dve.tensor_copy(y_tile[:, :], bank[:, 4, 0:C]).then_inc(y_sb, 1)

            last = dve.value_load(plan[0:1, 1, n_e - 1:n_e], min_val=0, max_val=TILES - 1)
            of_last = dve.value_load(plan[0:1, 0, n_e - 1:n_e], min_val=1, max_val=EM)
            dve.wait_ge(named(f"{pre}x_in"), (last + of_last) * 16 + 32)
            dve.wait_ge(y_out, (last + of_last) * 16 + 16)
            dve.tensor_copy(count[:, 0:1], tiles_upto[:, 0:1]).then_inc(named("all_out"), 1)

        def mix(k, pre, last):
            dve.wait_ge(named(f"{pre}got"), 16 * TOP * NT)
            for t in range(NT):
                step(dve.scalar_tensor_tensor(out=x_res[:, t, :], in0=y_got[:, 0, t, :], scalar=gates[:, 3, t:t + 1],
                                              in1=x_res[:, t, :], op0=ALU.mult, op1=ALU.add))
                dve.scalar_tensor_tensor(out=x_res[:, t, :], in0=y_got[:, 1, t, :], scalar=gates[:, 2, t:t + 1],
                                         in1=x_res[:, t, :], op0=ALU.mult, op1=ALU.add).then_inc(named(f"{pre}mix"), 1)
                dve.wait_ge(named(f"{pre}mix"), t + 1)
                if not last:
                    stats(x_res, t)

        def mlp():
            for t in range(NT):
                dve.wait_ge(named("ff_y"), t + 1)
                dve.tensor_tensor(x_res[:, t, :], x_res[:, t, :], bank[:, 4 + t % 2, 0:C],
                                  ALU.add).then_inc(named("ff_add"), 1)
                dve.wait_ge(named("ff_add"), t + 1)
                stats(x_res, t)

        dve.wait_ge(named("x_in"), 32)
        for t in range(NT):
            stats(x_res, t)
        normalize(0, x_res, 1e-6)
        qkv(0, "l0")
        attention(0, "l0")
        project(0, "l0", x_res)
        dve.wait_ge(named("l0proj_add"), NT)
        normalize(1, x_res, 1e-5, flat)
        gating(0, E0, FFC[0])
        routing(0, E0)
        output_bias(0)
        experts(0, "l0", E0)
        mix(0, "l0", False)
        normalize(2, x_res, 1e-6, flat)
        dve.wait_ge(named("xn"), 3 * NT)
        for t in range(NT):
            stats(flat, t)
        normalize(3, flat, 1e-5)
        qkv(1, "l1")
        attention(1, "l1")
        project(1, "l1", flat)
        dve.wait_ge(named("l1proj_add"), NT)
        normalize(4, flat, 1e-5)
        mlp()
        normalize(5, x_res, 1e-5, flat)
        gating(1, E1, FFC[2])
        routing(1, E1)
        output_bias(1)
        experts(1, "l1", E1)
        mix(1, "l1", True)

    @block.scalar
    def _(act):
        def root(k):
            act.wait_ge(named("var"), k + 1)
            act.activation(std[:, :], var_eps[:, :], ACT.Sqrt).then_inc(named("std"), 1)

        def to_xT(k, aff=None):
            if aff is not None:
                act.wait_ge(named("const"), 16)
            for t in range(NT):
                act.wait_ge(named("ln_tr"), LN_PE[k] + t + 1)
                tok = slice(t * P, (t + 1) * P)
                if aff is None:
                    ins = act.activation(xT[:, :, tok], bank[:, t % 4, 0:C].rearrange("p (c q) -> p c q", c=NC_),
                                         ACT.Copy)
                else:
                    for c in range(NC_):
                        ins = act.activation(xT[:, c, tok], bank[:, t % 4, c * P:(c + 1) * P], ACT.Identity,
                                             scale=affine[:, aff, 0, c:c + 1], bias=affine[:, aff, 1, c:c + 1])
                ins.then_inc(named("xT"), 1)

        def high_halves(n, pre):
            for t in range(NT):
                act.wait_ge(named(f"{pre}qk_tr"), t + 1)
                if t % 2 == 0 and t >= 4:
                    act.wait_ge(named(f"{pre}stack{t // 2 % 2}"), 16 * 24 * (t // 4))
                for i in range(2):
                    ins = act.activation(stage[:, t // 2 % 2, 2 * i, :, P * (t % 2):P * (t % 2) + P],
                                         bank[:, 6 + i, 0:C].rearrange("p (c q) -> p c q", c=NC_), ACT.Copy)
                ins.then_inc(named(f"{pre}hi"), 1)

        def softmax(n, pre):
            for i in range(2):
                act.wait_ge(named(f"{pre}stack{i}"), 16 * 24 * NQ // 2)
            for u in range(H * NT):
                act.wait_ge(named(f"{pre}st"), u + 1)
                if u >= P_RING:
                    act.wait_ge(named(f"{pre}pv"), u - P_RING + 1)
                act.activation(probs[:, u % P_RING, :], bank[:, 4:6, :].rearrange("p a b -> p (a b)"), ACT.Exp,
                               scale=SCALE).then_inc(named(f"{pre}exp"), 1)

        def mlp_gelu():
            act.wait_ge(named("ffc"), FFC[1])
            for v in range(NH):
                for f in range(NF):
                    act.wait_ge(named("ff_h"), NF * v + f + 1)
                    act.activation(hT[:, v, f, :], bank[:, f % 4, :], ACT.Gelu,
                                   bias=b1[:, E0 + E1, f:f + 1]).then_inc(named("ff_g"), 1)

        def experts(k, pre, n_e, func, row):
            act.wait_ge(named("plan"), k + 1)
            with act.Fori(0, n_e) as e:
                n_tiles = act.value_load(plan[0:1, 0, bass.ds(e, 1)], min_val=1, max_val=EM)
                first = act.value_load(plan[0:1, 1, bass.ds(e, 1)], min_val=0, max_val=TILES - 1)
                with act.Fori(0, n_tiles) as i:
                    for f in range(NF):
                        act.wait_ge(named(f"{pre}h"), (first + i) * NF + (f + 1))
                        act.activation(hT[:, 0, f, 0:P], bank[:, f % 4, 0:P], func,
                                       bias=b1[:, bass.ds(e + row, 1), f]).then_inc(named(f"{pre}g"), 1)

        def gap(k):
            act.wait_ge(named("gap"), k + 1)
            act.activation(gates[:, 1, :], gates[:, 0, :], ACT.Exp).then_inc(named("gap_exp"), 1)

        root(0)
        to_xT(0)
        high_halves(0, "l0")
        softmax(0, "l0")
        root(1)
        to_xT(1)
        gap(0)
        experts(0, "l0", E0, ACT.Gelu_apprx_tanh, 0)
        root(2)
        root(3)
        to_xT(3, 0)
        high_halves(1, "l1")
        softmax(1, "l1")
        root(4)
        to_xT(4, 1)
        mlp_gelu()
        root(5)
        to_xT(5)
        gap(1)
        experts(1, "l1", E1, ACT.Gelu, E0)

    @block.tensor
    def _(pe):
        def transposes(k):
            pe.wait_ge(named("ident"), 1)
            for t in range(NT):
                pe.wait_ge(named("xn"), XN[k] + t + 1)
                if t >= 4:
                    pe.wait_ge(named("xT"), LN_PE[k] + t - 3)
                tile = flat[:, t, :] if k in (1, 5) else xn[:, t % 2, :]
                for c in range(NC_):
                    ins = pe.transpose(bank[:, t % 4, c * P:(c + 1) * P], tile[:, c * P:(c + 1) * P], ident[:, :])
                ins.then_inc(named("ln_tr"), 1)
            pe.wait_ge(named("xT"), LN_PE[k] + NT)

        def qkv(n, pre):
            pe.wait_ge(named(f"{pre}w"), 32)
            for t in range(NT + 1):
                if t < NT:
                    b = 3 * (t % 2)
                    if t >= 2:
                        pe.wait_ge(named(f"{pre}v"), t - 1)
                    for i in range(3):
                        for c in range(NC_):
                            ins = pe.matmul(bank[:, b + i, 0:C], xT[:, c, t * P:(t + 1) * P],
                                            w_qkv[:, c, C * i:C * i + C], start=(c == 0), stop=(c == NC_ - 1))
                    ins.then_inc(named(f"{pre}qkv_mm"), 1)
                if t:
                    u = t - 1
                    pe.wait_ge(named(f"{pre}qk"), u + 1)
                    if u:
                        pe.wait_ge(named(f"{pre}lo"), u)
                    for i in range(2):
                        for c in range(NC_):
                            ins = pe.transpose(bank[:, 6 + i, c * P:(c + 1) * P],
                                               qk_tok[:, C * i + c * P:C * i + c * P + P], ident[:, :])
                    ins.then_inc(named(f"{pre}qk_tr"), 1)
            pe.wait_ge(named(f"{pre}lo"), NT)
            pe.wait_ge(named(f"{pre}v"), NT)

        def attention(n, pre):
            order = maxima_order()
            at = [0]
            for i in range(2):
                pe.wait_ge(named(f"{pre}stack{i}"), 16 * 24 * NQ // 2)
            pe.wait_ge(named("ones"), 2 * (n + 1))
            if n:
                pe.wait_ge(named("bias_of"), H)

            def maxima(count):
                for _ in range(count):
                    if at[0] == len(order):
                        return
                    kind, h, t = order[at[0]]
                    if at[0] >= 2:
                        was, h2, t2 = order[at[0] - 2]
                        if was == "tile":
                            pe.wait_ge(named(f"{pre}mx_read"), NT * h2 + t2 + 1)
                        else:
                            pe.wait_ge(named(f"{pre}shift"), h2 + 1)
                    pair = 2 * (at[0] % 2)
                    tok = slice(t * P, (t + 1) * P)
                    if kind == "tile":
                        own = t // (HALF // P)
                        for half in range(NH):
                            diag = n and half == own
                            ins = pe.matmul(bank[:, pair + half, :], q_stack[0:ROW_MAX, h, tok],
                                            k_stack[0:ROW_MAX, h, half * HALF:half * HALF + HALF],
                                            start=True, stop=not diag)
                            if diag:
                                o = t * P - own * HALF
                                ins = pe.matmul(bank[:, pair + half, o:o + P], bias_of[:, h, :], key_of[:, :],
                                                start=False, stop=True)
                    else:
                        pe.wait_ge(named(f"{pre}neg"), h + 1)
                        ins = pe.transpose(bank[0:NT, pair, 0:P], neg_max[:, h, :], ident[:, :])
                    ins.then_inc(named(f"{pre}mx_mm"), 1)
                    at[0] += 1

            def values(u):
                h, kt = divmod(u, NT)
                pe.wait_ge(named(f"{pre}exp"), u + 1)
                if kt == 0 and h >= 2:
                    pe.wait_ge(named(f"{pre}att"), NH * (h - 1))
                for half in range(NH):
                    b = 6 + (h + half) % 2
                    p = probs[:, u % P_RING, half * HALF:half * HALF + HALF]
                    o = 64 * half
                    pe.matmul(bank[o:o + D, b, :], v_tok[:, kt, D * h:D * h + D], p,
                              start=(kt == 0), stop=(kt == NT - 1))
                    ins = pe.matmul(bank[o + D:o + 2 * D, b, :], ones_v[:, :], p,
                                    start=(kt == 0), stop=(kt == NT - 1))
                ins.then_inc(named(f"{pre}pv"), 1)

            maxima(LEAD)
            for u in range(H * NT):
                h, kt = divmod(u, NT)
                if kt == 0:
                    pe.wait_ge(named(f"{pre}shifted{h % 2}"), 16 * (h // 2 + 1))
                if u:
                    pe.wait_ge(named(f"{pre}exp"), u)
                own = kt // (HALF // P)
                for half in range(NH):
                    diag = n and half == own
                    ins = pe.matmul(bank[:, 4 + half, :], k_stack[0:ROW_MAX + 1, h, kt * P:(kt + 1) * P],
                                    q_stack[0:ROW_MAX + 1, h, half * HALF:half * HALF + HALF],
                                    start=True, stop=not diag)
                    if diag:
                        o = kt * P - own * HALF
                        ins = pe.matmul(bank[:, 4 + half, o:o + P], key_of[:, :], bias_of[:, h, :],
                                        start=False, stop=True)
                ins.then_inc(named(f"{pre}st"), 1)
                maxima(1 + (kt == 0))
                if u:
                    values(u - 1)
            values(H * NT - 1)

        def project(n, pre):
            pe.wait_ge(named(f"{pre}att"), NH * H)
            pe.wait_ge(named(f"{pre}w2"), 32)
            for t in range(NT):
                if t >= 4:
                    pe.wait_ge(named(f"{pre}proj_add"), t - 3)
                for c in range(NC_):
                    ins = pe.matmul(bank[:, t % 4, 0:C], attT[:, c, t * P:(t + 1) * P], w_o[:, c, :],
                                    start=(c == 0), stop=(c == NC_ - 1))
                ins.then_inc(named(f"{pre}proj"), 1)

        def gating(k, n_e, ffc):
            pe.wait_ge(named("ffc"), ffc)
            for t in range(NT):
                if t >= 2:
                    pe.wait_ge(named("gate_top"), NT * k + t - 1)
                for c in range(NC_):
                    ins = pe.matmul(bank[:, 4 + t % 2, 0:n_e], xT[:, c, t * P:(t + 1) * P], w_gate[:, c, 0:n_e],
                                    start=(c == 0), stop=(c == NC_ - 1))
                ins.then_inc(named("gate_mm"), 1)
            pe.wait_ge(named("routed"), k + 1)
            rhs = routed[:, :, :].rearrange("p t e -> p (t e)")
            pe.matmul(bank[:, 4, 0:NT * EM], tri[:, :], rhs, start=True, stop=True)
            pe.matmul(bank[:, 5, 0:NT * EM], ones[:, :], rhs, start=True, stop=True).then_inc(named("counted"), 1)
            pe.wait_ge(named("slots"), k + 1)
            pe.wait_ge(named("comb"), k + 1)
            for t in range(NT):
                if t >= 2:
                    pe.wait_ge(named("combT"), NT * k + t - 1)
                pe.transpose(bank[0:EM, 4 + t % 2, 0:P], comb[:, t, :], ident[:, :]).then_inc(named("comb_tr"), 1)
            for t in range(NT):
                pe.wait_ge(named("combT"), NT * k + t + 1)
                if t >= 2:
                    pe.wait_ge(named("b2_add"), NT * k + t - 1)
                pe.matmul(bank[:, 6 + t % 2, 0:C], combT[0:n_e, t * P:(t + 1) * P], b2[0:n_e, :],
                          start=True, stop=True).then_inc(named("b2_mm"), 1)
            pe.wait_ge(named("b2_add"), NT * (k + 1))

        def experts(k, pre, n_e, flip):
            def turn():
                for c in range(NC_):
                    ins = pe.transpose(bank[:, 6, c * P:(c + 1) * P], x_tile[:, c * P:(c + 1) * P], ident[:, :])
                ins.then_inc(named(f"{pre}x_tr"), 1)

            pe.wait_ge(named(f"{pre}x_in"), 16)
            turn()
            pe.wait_ge(named("plan"), k + 1)
            with pe.Fori(0, n_e // 2) as pair:
                for s in range(2):
                    w1_, w2_ = w1[s ^ flip], w2[s ^ flip]
                    n_tiles = pe.value_load(plan[0:1, 0, bass.ds(pair * 2 + s, 1)], min_val=1, max_val=EM)
                    first = pe.value_load(plan[0:1, 1, bass.ds(pair * 2 + s, 1)], min_val=0, max_val=TILES - 1)
                    with pe.Fori(0, n_tiles) as i:
                        g = first + i
                        pe.wait_ge(named(f"{pre}w{s}_"), pair * 32 + 32)
                        pe.wait_ge(named(f"{pre}xT_sb"), g + 1)
                        for f in range(NF):
                            if f >= 4:
                                pe.wait_ge(named(f"{pre}g"), g * NF + (f - 3))
                            for c in range(NC_):
                                ins = pe.matmul(bank[:, f % 4, 0:P], w1_[:, c, f * P:(f + 1) * P],
                                                xT_tile[:, c, :], start=(c == 0), stop=(c == NC_ - 1))
                            ins.then_inc(named(f"{pre}h"), 1)
                        pe.wait_ge(named(f"{pre}x_in"), g * 16 + 32)
                        turn()
                        pe.wait_ge(named(f"{pre}y_sb"), g + 1)
                        for f in range(NF):
                            pe.wait_ge(named(f"{pre}g"), g * NF + (f + 1))
                            ins = pe.matmul(bank[:, 4, 0:C], hT[:, 0, f, 0:P], w2_[:, f, :],
                                            start=(f == 0), stop=(f == NF - 1))
                        ins.then_inc(named(f"{pre}y_mm"), 1)

        def mlp():
            pe.wait_ge(named("ffc"), FFC[1])
            pe.wait_ge(named("tables"), 12)
            pe.wait_ge(named("mlpw"), 32)

            def hidden(half):
                for f in range(NF):
                    if half or f >= 4:
                        pe.wait_ge(named("ff_g"), NF * half + f - 3)
                    for c in range(NC_):
                        ins = pe.matmul(bank[:, f % 4, :], w1[0][:, c, f * P:(f + 1) * P],
                                        xT[:, c, half * HALF:half * HALF + HALF], start=(c == 0), stop=(c == NC_ - 1))
                    ins.then_inc(named("ff_h"), 1)

            def outputs(half):
                for i in range(NT // NH):
                    t = NT // NH * half + i
                    if t >= 2:
                        pe.wait_ge(named("ff_add"), t - 1)
                    pe.matmul(bank[:, 4 + t % 2, 0:C], ones_row[:, :], b2[0:1, :], start=True, stop=False)
                    for f in range(NF):
                        if i == 0:
                            pe.wait_ge(named("ff_g"), NF * half + f + 1)
                        ins = pe.matmul(bank[:, 4 + t % 2, 0:C], hT[:, half, f, i * P:(i + 1) * P],
                                        w2[0][:, f, :], start=False, stop=(f == NF - 1))
                    ins.then_inc(named("ff_y"), 1)

            hidden(0)
            hidden(1)
            outputs(0)
            outputs(1)

        transposes(0)
        qkv(0, "l0")
        attention(0, "l0")
        project(0, "l0")
        transposes(1)
        gating(0, E0, FFC[0])
        experts(0, "l0", E0, 0)
        transposes(3)
        qkv(1, "l1")
        attention(1, "l1")
        project(1, "l1")
        transposes(4)
        mlp()
        transposes(5)
        gating(1, E1, FFC[2])
        experts(1, "l1", E1, 1)


def kernel(**inputs):
    import concourse.bacc as bacc
    from concourse.bass_utils import run_bass_kernel_spmd

    i = {k: np.asarray(v) for k, v in inputs.items()}

    def turned(w):
        return np.ascontiguousarray(np.swapaxes(w, -1, -2))

    def by_channel(v, n):
        return np.ascontiguousarray(np.moveaxis(v.reshape(v.shape[:-1] + (n, P)), -1, 0))

    half = D // 2
    pair = np.arange(ROPE, dtype=np.float32)
    angles = np.arange(T, dtype=np.float32)[:, None] / (np.float32(10000.0) ** (np.float32(2.0) * pair / np.float32(D)))
    trig = np.stack([np.cos(angles), np.sin(angles)]).astype(np.float32).reshape(2, NT, P, ROPE).transpose(2, 0, 1, 3)

    arrays = {
        "x": i["x"].reshape(T, C),
        "trig": trig,
        "affine": np.stack([by_channel(np.stack([i["L1_conv_ln1_g"], i["L1_conv_ln1_b"]]), NC_),
                            by_channel(np.stack([i["L1_conv_ln3_g"], i["L1_conv_ln3_b"]]), NC_)], axis=1),
        "l0qkv": turned(i["L0_conv_qkv_w"]), "l0bqkv": i["L0_conv_qkv_b"],
        "l0wo": turned(i["L0_conv_proj_w"]), "l0bo": i["L0_conv_proj_b"],
        "l0gate_w": turned(i["L0_ffn_gate_w"]), "l0gate_b": i["L0_ffn_gate_b"],
        "l0w1": turned(i["L0_ffn_w_fc"]), "l0w2": turned(i["L0_ffn_w_proj"]), "l0b2": i["L0_ffn_b_proj"],
        "b1": by_channel(np.concatenate([i["L0_ffn_b_fc"], i["L1_ffn_b1"], i["L1_conv_b1"][None]]), NF),
        "l1qkv": np.concatenate([i["L1_conv_wq"], i["L1_conv_wk"], i["L1_conv_wv"]], axis=1),
        "l1bqkv": np.concatenate([i["L1_conv_bq"], i["L1_conv_bk"], i["L1_conv_bv"]]),
        "l1wo": i["L1_conv_wo"], "l1bo": i["L1_conv_bo"],
        "attn_biases": turned(i["L1_conv_attn_biases"]),
        "mlp_w1": i["L1_conv_w1"], "mlp_w2": i["L1_conv_w2"], "mlp_b2": i["L1_conv_b2"][None],
        "l1gate_w": i["L1_ffn_gate_w"], "l1gate_b": i["L1_ffn_gate_b"],
        "l1w1": i["L1_ffn_w1"], "l1w2": i["L1_ffn_w2"], "l1b2": i["L1_ffn_b2"],
    }
    nc = bacc.Bacc("TRN2", target_bir_lowering=False, num_devices=1)
    arrays = {f"in_{k}": np.ascontiguousarray(v) for k, v in arrays.items()}
    aps = {k[3:]: nc.dram_tensor(k, v.shape, mybir.dt.from_np(v.dtype), kind="ExternalInput").ap()
           for k, v in arrays.items()}
    out = nc.dram_tensor("out_x", (T, C), F32, kind="ExternalOutput").ap()
    build(nc, aps, out)
    r = run_bass_kernel_spmd(nc, [arrays], core_ids=[0])
    return r.results[0]["out_x"].reshape(1, 32, 32, C)
```

```python
from contextlib import ExitStack

import numpy as np
import concourse.bass as bass
from concourse import mybir

F32 = mybir.dt.float32
F32R = mybir.dt.float32r
BF16 = mybir.dt.bfloat16
U32 = mybir.dt.uint32
I32 = mybir.dt.int32
ALU = mybir.AluOpType
ACT = mybir.ActivationFunctionType
AX = mybir.AxisListType

P = 128
T = 1024
C = 384
W = C + 1
F = 1536
NT = T // P
NC_ = C // P
NF = F // P
H = 12
D = C // H
HPC = P // D
SCALE = float(D) ** -0.5
HALF = 512
NH = T // HALF
S = 32
V = P // S
ROPE = 8
E0, E1 = 8, 6
EM = 8
TOP = 2
TILES = (TOP * T + (P - 1) * EM) // P
CLEARED = TILES + 2
SLOTS = (TILES + EM + 1) * P
QUARTER = 256
NQ = T // QUARTER
HEADS = (0, 4, 8, 1, 2, 3, 5, 6, 7, 9, 10, 11)
DONE_AT = (5, 8, 11)
ROW_MAX = 96
P_RING = 3
LEAD = 14
NEG = 2


def build(nc, a, out):
    with ExitStack() as ctx:
        program(nc, a, out, ctx)


def maxima_order():
    order = []
    for h in range(H):
        for t in range(NT):
            order.append(("tile", h, t))
            if h and t == NEG - 1:
                order.append(("turn", h - 1, 0))
    order.append(("turn", H - 1, 0))
    return order


def program(nc, a, out, ctx):
    def sb(name, shape, dt=F32, where=ctx):
        return where.enter_context(nc.sbuf_tensor(name, shape, dt))

    def sem(name):
        return ctx.enter_context(nc.semaphore(name))

    grouped = [nc.dram_tensor(f"grouped{n}", (SLOTS, W), F32, kind="Internal").ap() for n in range(2)]
    token_out = nc.dram_tensor("token_out", (TOP * T + P, C), F32, kind="Internal").ap()

    LN_PE = {0: 0, 1: NT, 3: 2 * NT, 4: 3 * NT, 5: 4 * NT}
    XN = {k: NT * k for k in range(6)}

    x_res = sb("x_res", [P, NT, C])
    rows = sb("rows", [P, NT, W])
    flat = rows[:, :, 0:C]
    row_id = rows[:, :, C:W].bitcast(I32)
    xT = sb("xT", [P, NC_, T])
    xn = sb("xn", [P, 2, C])
    ident = sb("ident", [P, P])
    bn_raw = sb("bn_raw", [P, NT, 6])
    bn_mv = sb("bn_mv", [P, NT, 2])
    var_eps = sb("var_eps", [P, NT])
    std = sb("std", [P, NT])
    rstd0 = sb("rstd0", [P, NT])
    newton = sb("newton", [P, NT])
    rstd = sb("rstd", [P, NT])
    affine = sb("affine", [P, 2, 2, NC_])
    tri = sb("tri", [P, P])
    ones = sb("ones", [P, P])
    lanes = sb("lanes", [P, EM])
    limits = sb("limits", [P, EM - 1])
    ids = sb("ids", [P, TOP, NT], I32)
    attT = xT

    with ExitStack() as att:
        q_stack = sb("q_stack", [P, H, T], F32R, att)
        k_stack = sb("k_stack", [P, H, T], F32R, att)
        v_tok = sb("v_tok", [P, NT, C], F32, att)
        w_o = sb("w_o", [P, NC_, C], F32, att)
        b_o = sb("b_o", [P, C], F32, att)
        ones_v = sb("ones_v", [P, D], F32, att)
        neg_max = sb("neg_max", [P, H, NT], F32, att)
        row_max = sb("row_max", [P, H, NT], F32, att)
        variate = sb("variate", [P, 12, H], F32, att)
        key_of = sb("key_of", [P, P], BF16, att)
        bias_of = sb("bias_of", [P, H, P], BF16, att)
        trig = sb("trig", [P, 2, NT, ROPE], F32, att)
        shift = sb("shift", [NT, 2, P], F32R, att)
        with ExitStack() as early:
            w_qkv = sb("w_qkv", [P, NC_, 3 * C], F32, early)
            b_qkv = sb("b_qkv", [P, 3 * C], F32, early)
            stage = sb("stage", [P, 2, 4, NC_, QUARTER], F32R, early)
            qk_tok = sb("qk_tok", [P, 2 * C], F32, early)
            rot = sb("rot", [P, 4, H, ROPE], F32, early)
        probs = sb("probs", [P, P_RING, T], F32, att)
        den = sb("den", [P, NC_, T], F32, att)

    with ExitStack() as ff:
        w1 = [sb(f"w1_{i}", [P, NC_, F], F32, ff) for i in range(2)]
        w2 = [sb(f"w2_{i}", [P, NF, C], F32, ff) for i in range(2)]
        hT = sb("hT", [P, 2, NF, HALF], F32, ff)
        x_tile = sb("x_tile", [P, W], F32, ff)
        x_id = x_tile[:, C:W].bitcast(I32)
        id_next = sb("id_next", [P, 1], I32, ff)
        id_held = sb("id_held", [P, 1], I32, ff)
        id_out = sb("id_out", [P, 1], I32, ff)
        xT_tile = sb("xT_tile", [P, NC_, P], F32, ff)
        y_tile = sb("y_tile", [P, C], F32, ff)
        y_got = sb("y_got", [P, TOP, NT, C], F32, ff)
        pick = sb("pick", [P, TOP, NT, EM], F32, ff)
        routed = sb("routed", [P, NT, EM], F32, ff)
        total = sb("total", [P, EM, NT], F32, ff)
        upto = sb("upto", [P, EM, NT], F32, ff)
        before = sb("before", [P, EM, NT], F32, ff)
        count = sb("count", [P, EM], F32, ff)
        filled = sb("filled", [P, EM, EM - 1], F32, ff)
        tiles = sb("tiles", [P, 2, EM], F32, ff)
        tiles_upto = sb("tiles_upto", [P, EM], F32, ff)
        offset = sb("offset", [P, EM], F32, ff)
        place = sb("place", [P, NT, EM], F32, ff)
        picked = sb("picked", [P, TOP, NT, EM], F32, ff)
        slot_f = sb("slot_f", [P, TOP, NT], F32, ff)
        slot = sb("slot", [P, TOP, NT], U32, ff)
        plan = sb("plan", [1, 2, EM], mybir.dt.int32, ff)
        b1 = sb("b1", [P, 15, NF], F32, ff)
        b2 = sb("b2", [8, C], F32, ff)
        w_gate = sb("w_gate", [P, NC_, 8], F32, ff)
        b_gate = sb("b_gate", [P, 8], F32, ff)
        scores = sb("scores", [P, NT, 8], F32, ff)
        top = sb("top", [P, NT, 8], F32, ff)
        top_i = sb("top_i", [P, NT, 8], U32, ff)
        top_f = sb("top_f", [P, NT, 2], F32, ff)
        gates = sb("gates", [P, 4, NT], F32, ff)
        comb = sb("comb", [P, NT, 8], F32, ff)
        comb2 = sb("comb2", [P, NT, 8], F32, ff)
        combT = sb("combT", [8, T], F32, ff)
        ones_row = ones[0:1, :]

    bank = ctx.enter_context(nc.psum_tensor("bank", [P, 8, HALF], F32))

    G = {}

    def named(name):
        if name not in G:
            G[name] = sem(name)
        return G[name]

    loads = {}

    block = ctx.enter_context(nc.Block())

    @block.sync
    def _(sp):
        def load(name, dst, src):
            sp.dma_start(dst, src).then_inc(named(name), 16)
            loads[name] = loads.get(name, 0) + 16

        def attention_weights(n, pre):
            load(f"{pre}w", w_qkv[:, :, :], a[f"{pre}qkv"].rearrange("(c p) n -> p c n", p=P))
            load(f"{pre}w", b_qkv[:, :], a[f"{pre}bqkv"].partition_broadcast(P))
            load(f"{pre}w2", w_o[:, :, :], a[f"{pre}wo"].rearrange("(c p) n -> p c n", p=P))
            load(f"{pre}w2", b_o[:, :], a[f"{pre}bo"].partition_broadcast(P))

        def stacks(n, pre):
            for qr in range(NQ):
                sp.wait_ge(named(f"{pre}lo"), 2 * (qr + 1))
                tok = slice(qr * QUARTER, (qr + 1) * QUARTER)
                for j in range(HPC):
                    done = named(f"{pre}stack{qr % 2}" if j else f"{pre}first{qr % 2}")
                    for stack, rows, kind in ((q_stack, 0, 0), (q_stack, 1, 1), (q_stack, 2, 0),
                                              (k_stack, 0, 2), (k_stack, 1, 2), (k_stack, 2, 3)):
                        sp.dma_start(stack[D * rows:D * rows + D, j:H:HPC, tok].bitcast(F32),
                                     stage[D * j:D * j + D, qr % 2, kind, :, :].bitcast(F32)).then_inc(done, 16)
            for h in range(H):
                sp.wait_ge(named(f"{pre}shift"), h + 1)
                sp.dma_start(q_stack[ROW_MAX:ROW_MAX + 1, HEADS[h], :].rearrange("p (t q) -> p t q", t=NT).bitcast(F32),
                             shift[:, h % 2, :].bitcast(F32)).then_inc(named(f"{pre}shifted{h % 2}"), 16)

        def weights(name, at, w1_src, w2_src):
            sp.dma_start(w1[at][:, :, :], w1_src.rearrange("(c p) n -> p c n", p=P)).then_inc(named(name), 16)
            sp.dma_start(w2[at][:, :, :], w2_src.rearrange("(c p) n -> p c n", p=P)).then_inc(named(name + "2"), 16)

        def later_experts(pre, n_e, flip):
            src1 = a[f"{pre}w1"].rearrange("e k n -> (e k) n")
            src2 = a[f"{pre}w2"].rearrange("e k n -> (e k) n")
            sp.wait_ge(named("plan"), 1 + (pre == "l1"))
            with sp.Fori(1, n_e // 2) as pair:
                for s in range(2):
                    e = pair * 2 + s
                    through = sp.value_load(plan[0:1, 1, bass.ds(e - 1, 1)], min_val=1, max_val=TILES)
                    rows1 = src1[bass.ds(e * C, C), :]
                    rows2 = src2[bass.ds(e * F, F), :]
                    sp.wait_ge(named(f"{pre}y_mm"), through)
                    weights(f"{pre}w{s}_", s ^ flip, rows1, rows2)

        def collect(n, pre):
            sp.wait_ge(named("all_out"), n + 1)
            for q in range(NT // 2):
                for j in range(TOP):
                    r = T * j + 2 * P * q
                    sp.dma_start(y_got[:, j, 2 * q:2 * q + 2, :],
                                 token_out[r:r + 2 * P, :].rearrange("(t p) c -> p t c", p=P)
                                 ).then_inc(named(f"{pre}got{q}"), 16)

        for half in range(2):
            load("x_in", x_res[:, 4 * half:4 * half + 4, :],
                 a["x"][half * HALF:half * HALF + HALF, :].rearrange("(t p) c -> p t c", p=P))
        load("const", affine[:, :, :, :], a["affine"])
        attention_weights(0, "l0")
        stacks(0, "l0")
        sp.wait_ge(named("l0proj_add"), NT)
        load("ffc", b1[:, :, :], a["b1"])
        load("ffc", b2[:, :], a["l0b2"])
        load("ffc", w_gate[:, :, :], a["l0gate_w"].rearrange("(c p) n -> p c n", p=P))
        load("ffc", b_gate[:, :], a["l0gate_b"].partition_broadcast(P))
        for s in range(2):
            weights(f"l0w{s}_", s, a["l0w1"][s], a["l0w2"][s])
        later_experts("l0", E0, 0)
        collect(0, "l0")
        sp.wait_ge(named("l0mix"), NT)
        attention_weights(1, "l1")
        load("l1trig", trig[:, :, :, :], a["trig"])
        load("l1bias", variate[:, 0:2, :], a["attn_biases"].partition_broadcast(P))
        stacks(1, "l1")
        sp.wait_ge(named("l1proj_add"), NT)
        load("ffc", b1[:, :, :], a["b1"])
        load("ffc", b2[0:1, :], a["mlp_b2"])
        weights("mlpw", 0, a["mlp_w1"], a["mlp_w2"])
        weights("l1w0_", 1, a["l1w1"][0], a["l1w2"][0])
        sp.wait_ge(named("ff_add"), NT)
        load("ffc", b2[0:E1, :], a["l1b2"])
        load("ffc", w_gate[:, :, 0:E1], a["l1gate_w"].rearrange("(c p) n -> p c n", p=P))
        load("ffc", b_gate[:, 0:E1], a["l1gate_b"].partition_broadcast(P))
        weights("l1w1_", 0, a["l1w1"][1], a["l1w2"][1])
        later_experts("l1", E1, 1)
        collect(1, "l1")
        for t in range(NT):
            sp.wait_ge(named("l1mix"), t + 1)
            sp.dma_start(out[t * P:(t + 1) * P, :], x_res[:, t, :]).then_inc(named("stored"), 16)
        sp.wait_ge(named("stored"), 16 * NT)

    TABLES = 8
    FFC = [64, 96, 144]

    def variate_tables(pool):
        done = named("vt")
        n = [0]

        def step(ins):
            n[0] += 1
            ins.then_inc(done, 1)
            pool.wait_ge(done, n[0])

        pool.wait_ge(named("l1bias"), 16)
        diff, p1, p2, p3 = (variate[:, i, :] for i in (2, 3, 4, 5))
        r1, r2 = (variate[:, i, :] for i in (6, 7))
        step(pool.tensor_tensor(diff, variate[:, 0, :], variate[:, 1, :], ALU.subtract))
        step(pool.tensor_scalar(diff, diff, float(D) ** 0.5, 0.0, ALU.mult, ALU.add))
        pieces = bias_of[:, 0, 0:3 * H].rearrange("p (i h) -> p i h", i=3)
        step(pool.tensor_copy(pieces[:, 0, :], diff))
        step(pool.tensor_copy(p1, pieces[:, 0, :]))
        step(pool.tensor_tensor(r1, diff, p1, ALU.subtract))
        step(pool.tensor_copy(pieces[:, 1, :], r1))
        step(pool.tensor_copy(p2, pieces[:, 1, :]))
        step(pool.tensor_tensor(r2, r1, p2, ALU.subtract))
        step(pool.tensor_copy(pieces[:, 2, :], r2))
        step(pool.tensor_copy(p3, pieces[:, 2, :]))
        own = variate[:, 8, :]
        for i, piece in ((9, p1), (10, p2), (11, p3)):
            lo = V * (i - 9)
            step(pool.affine_select(out=variate[:, i, :], in_=piece, compare_op=ALU.is_ge, fill=0.0, base=-lo,
                                    pattern=[[0, H]], channel_multiplier=1))
            step(pool.affine_select(out=variate[:, i, :], in_=variate[:, i, :], compare_op=ALU.is_ge, fill=0.0,
                                    base=lo + V - 1, pattern=[[0, H]], channel_multiplier=-1))
        step(pool.tensor_tensor(own, variate[:, 9, :], variate[:, 10, :], ALU.add))
        step(pool.tensor_tensor(own, own, variate[:, 11, :], ALU.add))
        step(pool.memset(key_of[:, :], 0.0))
        for i in range(3):
            for v in range(V):
                step(pool.affine_select(out=key_of[:, S * v:S * v + S], in_=key_of[:, S * v:S * v + S],
                                        compare_op=ALU.not_equal, fill=1.0, base=-(V * i + v),
                                        pattern=[[0, S]], channel_multiplier=1))
        for h in range(H):
            pool.tensor_scalar(bias_of[:, h, :], key_of[:, :], own[:, h:h + 1], None,
                               ALU.mult).then_inc(named("bias_of"), 1)

    def tables(pool):
        done = named("tables")
        pool.memset(tri[:, :], 0.0).then_inc(done, 1)
        pool.wait_ge(done, 1)
        pool.affine_select(out=tri[:, :], in_=tri[:, :], compare_op=ALU.is_ge, fill=1.0, base=0,
                           pattern=[[-1, P]], channel_multiplier=1).then_inc(done, 1)
        pool.memset(ones[:, :], 1.0).then_inc(done, 1)
        pool.iota(lanes[:, :], pattern=[[1, EM]], base=0, channel_multiplier=0,
                  allow_small_or_imprecise_dtypes=True).then_inc(done, 1)
        pool.iota(limits[:, :], pattern=[[P, EM - 1]], base=P, channel_multiplier=0,
                  allow_small_or_imprecise_dtypes=True).then_inc(done, 1)
        pool.iota(ids[:, :, :], pattern=[[T, TOP], [P, NT]], base=0, channel_multiplier=1).then_inc(done, 1)
        pool.memset(rows[:, 0, 0:C], 0.0).then_inc(done, 1)
        pool.iota(row_id[:, 0, :], pattern=[[0, 1]], base=TOP * T, channel_multiplier=1).then_inc(done, 1)
        pool.wait_ge(done, TABLES)

    def clear(pool):
        for n in range(2):
            pool.dma_start(grouped[n][0:CLEARED * P, :].rearrange("(t p) c -> p t c", p=P),
                           rows[:, 0, :].unsqueeze(1).to_broadcast([P, CLEARED, W])).then_inc(named("cleared"), 16)

    def exchange(pool, n, pre, n_e):
        pool.memset(y_tile[:, :], 0.0).then_inc(named("y_zero"), 1)
        pool.iota(id_out[:, :], pattern=[[0, 1]], base=TOP * T, channel_multiplier=1).then_inc(named("y_zero"), 1)
        pool.wait_ge(named("slots"), n + 1)
        for j in range(TOP):
            if j:
                pool.wait_ge(named("second_id"), n + 1)
            for t in range(NT):
                pool.indirect_dma_start(grouped[n][:, :], bass.IndirectOffsetOnAxis(ap=slot[:, j, t:t + 1], axis=0),
                                        rows[:, t, :], None).then_inc(named(f"{pre}sent"), 16)
        pool.wait_ge(named(f"{pre}sent"), 16 * TOP * NT)
        def send_y():
            pool.indirect_dma_start(token_out[:, :], bass.IndirectOffsetOnAxis(ap=id_out[:, 0:1], axis=0),
                                    y_tile[:, :], None).then_inc(named(f"{pre}y_out"), 16)

        loaded, read, y_sb = named(f"{pre}x_in"), named(f"{pre}x_read"), named(f"{pre}y_sb")
        pool.dma_start(x_tile[:, :], grouped[n][0:P, :]).then_inc(loaded, 16)
        pool.wait_ge(named("y_zero"), 2 * n + 2)
        pool.wait_ge(read, 1)
        pool.dma_start(x_tile[:, :], grouped[n][P:2 * P, :]).then_inc(loaded, 16)
        with pool.Fori(0, n_e) as e:
            n_tiles = pool.value_load(plan[0:1, 0, bass.ds(e, 1)], min_val=1, max_val=EM)
            first = pool.value_load(plan[0:1, 1, bass.ds(e, 1)], min_val=0, max_val=TILES - 1)
            with pool.Fori(0, n_tiles) as i:
                g = first + i
                src = grouped[n][bass.ds(g * P + 2 * P, P), :]
                pool.wait_ge(read, g + 2)
                pool.wait_ge(y_sb, g + 1)
                pool.dma_start(x_tile[:, :], src).then_inc(loaded, 16)
                send_y()
        pool.wait_ge(named("last_y"), n + 1)
        send_y()

    @block.gpsimd
    def _(pool):
        pool.memset(ident[:, :], 0.0).then_inc(named("id0"), 1)
        pool.wait_ge(named("id0"), 1)
        pool.affine_select(out=ident[:, :], in_=ident[:, :], compare_op=ALU.not_equal, fill=1.0, base=0,
                           pattern=[[-1, P]], channel_multiplier=1).then_inc(named("ident"), 1)
        pool.wait_ge(named("ident"), 1)
        tables(pool)
        for n, pre in enumerate(("l0", "l1")):
            if n:
                pool.wait_ge(named("l0mix"), NT)
            pool.memset(k_stack[ROW_MAX:ROW_MAX + 1, :, :].bitcast(F32), 1.0).then_inc(named("ones"), 1)
            pool.wait_ge(named("ones"), 2 * n + 1)
            pool.memset(ones_v[:, :], 1.0).then_inc(named("ones"), 1)
            if n:
                variate_tables(pool)
            pool.wait_ge(named("ones"), 2 * n + 2)
            acc = flat if n else x_res
            pool.wait_ge(named(f"{pre}w2"), 32)
            if not n:
                clear(pool)
            pool.wait_ge(named("xn"), NT * (4 if n else 1))
            for t in range(NT):
                pool.tensor_tensor(acc[:, t, :], acc[:, t, :], b_o[:, :], ALU.add).then_inc(named(f"{pre}bo"), 1)
            pool.wait_ge(named(f"{pre}proj_add"), NT)
            exchange(pool, n, pre, E1 if n else E0)

    @block.vector
    def _(dve):
        chain = [0]

        def step(ins):
            chain[0] += 1
            ins.then_inc(named("dve_chain"), 1)
            dve.wait_ge(named("dve_chain"), chain[0])

        def stats(src, t):
            step(dve.bn_stats(bn_raw[:, t, :], src[:, t, :]))
            dve.bn_aggr(bn_mv[:, t, :], bn_raw[:, t, :]).then_inc(named("stats"), 1)

        def normalize(k, src, eps, dst=None):
            dve.wait_ge(named("stats"), NT * (k + 1))
            dve.tensor_scalar(var_eps[:, :], bn_mv[:, :, 1], eps, None, ALU.add).then_inc(named("var"), 1)
            dve.wait_ge(named("std"), k + 1)
            step(dve.reciprocal(rstd0[:, :], std[:, :]))
            step(dve.tensor_tensor(newton[:, :], rstd0[:, :], rstd0[:, :], ALU.mult))
            step(dve.tensor_tensor(newton[:, :], newton[:, :], var_eps[:, :], ALU.mult))
            step(dve.tensor_scalar(newton[:, :], newton[:, :], -0.5, 1.5, ALU.mult, ALU.add))
            step(dve.tensor_tensor(rstd[:, :], newton[:, :], rstd0[:, :], ALU.mult))
            for t in range(NT):
                if k == 1 and t == 0:
                    dve.wait_ge(named("cleared"), 32)
                if dst is None:
                    if t >= 2:
                        dve.wait_ge(named("ln_tr"), LN_PE[k] + t - 1)
                to = dst[:, t, :] if dst is not None else xn[:, t % 2, :]
                dve.tensor_scalar(to, src[:, t, :], bn_mv[:, t, 0:1], rstd[:, t:t + 1],
                                  ALU.subtract, ALU.mult).then_inc(named("xn"), 1)

        def qkv(n, pre):
            dve.wait_ge(named(f"{pre}w"), 32)
            if n:
                dve.wait_ge(named("l1trig"), 16)
            for t in range(NT + 1):
                if t < NT:
                    b = 3 * (t % 2)
                    dve.wait_ge(named(f"{pre}qkv_mm"), t + 1)
                    if t:
                        dve.wait_ge(named(f"{pre}qk_tr"), t)
                    for i in range(2):
                        ins = dve.tensor_tensor(qk_tok[:, C * i:C * i + C], bank[:, b + i, 0:C],
                                                b_qkv[:, C * i:C * i + C], ALU.add)
                    if n:
                        step(ins)
                        ins = rope(t)
                    ins.then_inc(named(f"{pre}qk"), 1)
                    dve.tensor_tensor(v_tok[:, t, :], bank[:, b + 2, 0:C], b_qkv[:, 2 * C:3 * C],
                                      ALU.add).then_inc(named(f"{pre}v"), 1)
                if t:
                    u = t - 1
                    dve.wait_ge(named(f"{pre}hi"), u + 1)
                    if u % 2 == 0 and u >= 4:
                        dve.wait_ge(named(f"{pre}first{u // 2 % 2}"), 16 * 6 * (u // 4))
                        dve.wait_ge(named(f"{pre}stack{u // 2 % 2}"), 16 * 18 * (u // 4))
                    for i in range(2):
                        tok = slice(P * (u % 2), P * (u % 2) + P)
                        ins = dve.tensor_tensor(stage[:, u // 2 % 2, 2 * i + 1, :, tok],
                                                bank[:, 6 + i, 0:C].rearrange("p (c q) -> p c q", c=NC_),
                                                stage[:, u // 2 % 2, 2 * i, :, tok].bitcast(F32), ALU.subtract)
                    ins.then_inc(named(f"{pre}lo"), 1)

        def rope(t):
            cos = trig[:, 0, t, :].unsqueeze(1).to_broadcast([P, H, ROPE])
            sin = trig[:, 1, t, :].unsqueeze(1).to_broadcast([P, H, ROPE])
            for i in range(2):
                qk = qk_tok[:, C * i:C * i + C].rearrange("p (h d) -> p h d", h=H)
                x1, x2 = qk[:, :, 0:ROPE], qk[:, :, D // 2:D // 2 + ROPE]
                dve.tensor_tensor(rot[:, 0], x1, cos, ALU.mult)
                dve.tensor_tensor(rot[:, 1], x2, sin, ALU.mult)
                dve.tensor_tensor(rot[:, 2], x2, cos, ALU.mult)
                step(dve.tensor_tensor(rot[:, 3], x1, sin, ALU.mult))
                dve.tensor_tensor(x1, rot[:, 0], rot[:, 1], ALU.subtract)
                ins = dve.tensor_tensor(x2, rot[:, 2], rot[:, 3], ALU.add)
                if i == 0:
                    step(ins)
            return ins

        def attention(n, pre):
            order = maxima_order()
            at = [0]

            def maxima(count):
                for _ in range(count):
                    if at[0] == len(order):
                        return
                    kind, h, t = order[at[0]]
                    dve.wait_ge(named(f"{pre}mx_mm"), at[0] + 1)
                    pair = 2 * (at[0] % 2)
                    if kind == "tile":
                        ins = dve.tensor_reduce(row_max[:, h, t:t + 1], bank[:, pair:pair + 2, :], AX.XY, ALU.max)
                        ins.then_inc(named(f"{pre}mx_read"), 1)
                        if t == NT - 1:
                            dve.wait_ge(named(f"{pre}mx_read"), NT * (h + 1))
                            dve.tensor_scalar(neg_max[:, h, :], row_max[:, h, :], -1.0, None,
                                              ALU.mult).then_inc(named(f"{pre}neg"), 1)
                    else:
                        if h >= 2:
                            dve.wait_ge(named(f"{pre}shifted{h % 2}"), 16 * (h // 2))
                        dve.tensor_copy(shift[:, h % 2, :], bank[0:NT, pair, 0:P]).then_inc(named(f"{pre}shift"), 1)
                    at[0] += 1

            def divide(c, t):
                tok = slice(t * P, (t + 1) * P)
                step(dve.reciprocal(den[:, c, tok], den[:, c, tok]))
                dve.tensor_tensor(attT[:, c, tok], attT[:, c, tok], den[:, c, tok],
                                  ALU.mult).then_inc(named(f"{pre}att"), 1)

            maxima(LEAD)
            divided = 0
            for u in range(H * NT):
                maxima(1 + (u % NT == 0))
                c, t = divmod(divided, NT)
                if c < NC_ - 1 and u >= NT * (DONE_AT[c] + 1) + 6 + 2 * t:
                    dve.wait_ge(named(f"{pre}acc_copy"), 4 * (DONE_AT[c] + 1))
                    divide(c, t)
                    divided += 1
            maxima(len(order))
            dve.wait_ge(named(f"{pre}acc_copy"), 4 * H)
            for at_end in range(divided, NC_ * NT):
                divide(*divmod(at_end, NT))

        def project(n, pre, acc):
            for t in range(NT):
                dve.wait_ge(named(f"{pre}proj"), t + 1)
                dve.wait_ge(named(f"{pre}bo"), NT)
                dve.tensor_tensor(acc[:, t, :], acc[:, t, :], bank[:, t % 4, 0:C],
                                  ALU.add).then_inc(named(f"{pre}proj_add"), 1)
                dve.wait_ge(named(f"{pre}proj_add"), t + 1)
                if n:
                    step(dve.tensor_tensor(x_res[:, t, :], x_res[:, t, :], acc[:, t, :], ALU.add))
                stats(acc, t)

        def gating(k, n_e, ffc):
            dve.wait_ge(named("ffc"), ffc)
            dve.wait_ge(named("tables"), TABLES)
            if n_e < EM:
                step(dve.memset(scores[:, :, n_e:EM], -3.0e38))
            for t in range(NT):
                dve.wait_ge(named("gate_mm"), NT * k + t + 1)
                step(dve.tensor_tensor(scores[:, t, 0:n_e], bank[:, 4 + t % 2, 0:n_e], b_gate[:, 0:n_e], ALU.add))
                step(dve.max(top[:, t, :], scores[:, t, :]))
                dve.max_index(top_i[:, t, :], top[:, t, :], scores[:, t, :]).then_inc(named("gate_top"), 1)
            dve.wait_ge(named("gate_top"), NT * (k + 1))
            dve.tensor_tensor(gates[:, 0, :], top[:, :, 1], top[:, :, 0], ALU.subtract).then_inc(named("gap"), 1)
            step(dve.tensor_copy(top_f[:, :, :], top_i[:, :, 0:TOP]))

        def routing(k, n_e):
            wide = [P, NT, EM]
            for j in range(TOP):
                ins = dve.tensor_tensor(pick[:, j], lanes[:, :].unsqueeze(1).to_broadcast(wide),
                                        top_f[:, :, j].unsqueeze(2).to_broadcast(wide), ALU.is_equal)
            step(ins)
            dve.tensor_tensor(routed[:, :, :], pick[:, 0], pick[:, 1], ALU.add).then_inc(named("routed"), 1)
            dve.wait_ge(named("counted"), k + 1)
            step(dve.tensor_copy(total[:, :, :], bank[:, 5, 0:NT * EM].rearrange("p (t e) -> p e t", t=NT)))
            flat_et = lambda x: x[:, :, :].rearrange("p e t -> p (e t)")
            step(dve.tensor_tensor_scan(flat_et(upto), ones[:, 0:EM * NT], flat_et(total), 0.0, ALU.mult, ALU.add))
            step(dve.tensor_tensor(before[:, :, :], upto[:, :, :], total[:, :, :], ALU.subtract))
            step(dve.tensor_tensor(count[:, :], upto[:, :, NT - 1], before[:, :, 0], ALU.subtract))
            step(dve.tensor_tensor(filled[:, :, :], count[:, :].unsqueeze(2).to_broadcast([P, EM, EM - 1]),
                                   limits[:, :].unsqueeze(1).to_broadcast([P, EM, EM - 1]), ALU.is_gt))
            step(dve.tensor_reduce(tiles[:, 0, :], filled[:, :, :], AX.X, ALU.add))
            step(dve.tensor_scalar(tiles[:, 0, :], tiles[:, 0, :], 1.0, None, ALU.add))
            step(dve.tensor_tensor_scan(tiles_upto[:, :], ones[:, 0:EM], tiles[:, 0, :], 0.0, ALU.mult, ALU.add))
            step(dve.tensor_tensor(tiles[:, 1, :], tiles_upto[:, :], tiles[:, 0, :], ALU.subtract))
            dve.tensor_copy(plan[:, :, :], tiles[0:1, :, :]).then_inc(named("plan"), 1)
            step(dve.scalar_tensor_tensor(out=offset[:, :], in0=tiles[:, 1, :], scalar=float(P),
                                          in1=before[:, :, 0], op0=ALU.mult, op1=ALU.subtract))
            step(dve.tensor_tensor(place[:, :, :], before[:, :, :].rearrange("p e t -> p t e"),
                                   bank[:, 4, 0:NT * EM].rearrange("p (t e) -> p t e", t=NT), ALU.add))
            step(dve.tensor_tensor(place[:, :, :], place[:, :, :], offset[:, :].unsqueeze(1).to_broadcast(wide),
                                   ALU.add))
            for j in range(TOP):
                ins = dve.tensor_tensor(picked[:, j], pick[:, j], place[:, :, :], ALU.mult)
            step(ins)
            step(dve.tensor_reduce(slot_f[:, :, :], picked[:, :, :, :], AX.X, ALU.add))
            step(dve.tensor_copy(row_id[:, :, 0], ids[:, 0, :]))
            dve.tensor_copy(slot[:, :, :], slot_f[:, :, :]).then_inc(named("slots"), 1)

        def output_bias(k):
            dve.wait_ge(named("gap_exp"), k + 1)
            step(dve.tensor_scalar(gates[:, 2, :], gates[:, 1, :], 1.0, None, ALU.add))
            step(dve.reciprocal(gates[:, 3, :], gates[:, 2, :]))
            step(dve.tensor_tensor(gates[:, 2, :], gates[:, 1, :], gates[:, 3, :], ALU.mult))
            for j, gate in ((0, 3), (1, 2)):
                to = comb if j else comb2
                step(dve.tensor_tensor(to[:, :, :], pick[:, j],
                                       gates[:, gate, :].unsqueeze(2).to_broadcast([P, NT, EM]), ALU.mult))
            dve.tensor_tensor(comb[:, :, :], comb[:, :, :], comb2[:, :, :], ALU.add).then_inc(named("comb"), 1)
            dve.wait_ge(named(f"l{k}sent"), 16 * NT)
            dve.tensor_copy(row_id[:, :, 0], ids[:, 1, :]).then_inc(named("second_id"), 1)
            for t in range(NT):
                dve.wait_ge(named("comb_tr"), NT * k + t + 1)
                dve.tensor_copy(combT[:, t * P:(t + 1) * P], bank[0:EM, 4 + t % 2, 0:P]).then_inc(named("combT"), 1)
            for t in range(NT):
                dve.wait_ge(named("b2_mm"), NT * k + t + 1)
                dve.tensor_tensor(x_res[:, t, :], x_res[:, t, :], bank[:, 6 + t % 2, 0:C],
                                  ALU.add).then_inc(named("b2_add"), 1)
            dve.wait_ge(named("b2_add"), NT * (k + 1))

        def experts(k, pre, n_e):
            y_sb, y_out = named(f"{pre}y_sb"), named(f"{pre}y_out")

            def rows_in():
                return dve.tensor_copy(xT_tile[:, :, :], bank[:, 6, 0:C].rearrange("p (c q) -> p c q", c=NC_))

            dve.wait_ge(named(f"{pre}x_tr"), 1)
            rows_in().then_inc(named(f"{pre}xT_sb"), 1)
            dve.tensor_copy(id_next[:, :], x_id).then_inc(named(f"{pre}x_read"), 1)
            dve.wait_ge(named(f"{pre}x_read"), 1)
            dve.tensor_copy(id_held[:, :], id_next[:, :]).then_inc(y_sb, 1)
            dve.wait_ge(named("plan"), k + 1)
            with dve.Fori(0, n_e) as e:
                n_tiles = dve.value_load(plan[0:1, 0, bass.ds(e, 1)], min_val=1, max_val=EM)
                first = dve.value_load(plan[0:1, 1, bass.ds(e, 1)], min_val=0, max_val=TILES - 1)
                with dve.Fori(0, n_tiles) as i:
                    g = first + i
                    dve.wait_ge(named(f"{pre}x_tr"), g + 2)
                    rows_in().then_inc(named(f"{pre}xT_sb"), 1)
                    dve.wait_ge(y_sb, g + 1)
                    dve.tensor_copy(id_next[:, :], x_id).then_inc(named(f"{pre}x_read"), 1)
                    dve.wait_ge(named(f"{pre}y_mm"), g + 1)
                    dve.wait_ge(y_out, g * 16 + 16)
                    dve.tensor_copy(y_tile[:, :], bank[:, 4, 0:C])
                    dve.tensor_copy(id_out[:, :], id_held[:, :]).then_inc(named(f"{pre}id_out"), 1)
                    dve.wait_ge(named(f"{pre}id_out"), g + 1)
                    dve.tensor_copy(id_held[:, :], id_next[:, :]).then_inc(y_sb, 1)

            last = dve.value_load(plan[0:1, 1, n_e - 1:n_e], min_val=0, max_val=TILES - 1)
            of_last = dve.value_load(plan[0:1, 0, n_e - 1:n_e], min_val=1, max_val=EM)
            dve.wait_ge(y_sb, last + of_last + 1)
            dve.tensor_copy(count[:, 0:1], tiles_upto[:, 0:1]).then_inc(named("last_y"), 1)
            dve.wait_ge(named(f"{pre}x_in"), (last + of_last) * 16 + 32)
            dve.wait_ge(y_out, (last + of_last) * 16 + 16)
            dve.wait_ge(named("last_y"), k + 1)
            dve.tensor_copy(count[:, 0:1], tiles_upto[:, 0:1]).then_inc(named("all_out"), 1)

        def mix(k, pre, last):
            for t in range(NT):
                dve.wait_ge(named(f"{pre}got{t // 2}"), 32)
                step(dve.scalar_tensor_tensor(out=x_res[:, t, :], in0=y_got[:, 0, t, :], scalar=gates[:, 3, t:t + 1],
                                              in1=x_res[:, t, :], op0=ALU.mult, op1=ALU.add))
                dve.scalar_tensor_tensor(out=x_res[:, t, :], in0=y_got[:, 1, t, :], scalar=gates[:, 2, t:t + 1],
                                         in1=x_res[:, t, :], op0=ALU.mult, op1=ALU.add).then_inc(named(f"{pre}mix"), 1)
                dve.wait_ge(named(f"{pre}mix"), t + 1)
                if not last:
                    stats(x_res, t)

        def mlp():
            for t in range(NT):
                dve.wait_ge(named("ff_y"), t + 1)
                dve.tensor_tensor(x_res[:, t, :], x_res[:, t, :], bank[:, 4 + t % 2, 0:C],
                                  ALU.add).then_inc(named("ff_add"), 1)
                dve.wait_ge(named("ff_add"), t + 1)
                stats(x_res, t)

        dve.wait_ge(named("x_in"), 32)
        for t in range(NT):
            stats(x_res, t)
        normalize(0, x_res, 1e-6)
        qkv(0, "l0")
        attention(0, "l0")
        project(0, "l0", x_res)
        dve.wait_ge(named("l0proj_add"), NT)
        normalize(1, x_res, 1e-5, flat)
        gating(0, E0, FFC[0])
        routing(0, E0)
        output_bias(0)
        experts(0, "l0", E0)
        mix(0, "l0", False)
        normalize(2, x_res, 1e-6, flat)
        dve.wait_ge(named("xn"), 3 * NT)
        for t in range(NT):
            stats(flat, t)
        normalize(3, flat, 1e-5)
        qkv(1, "l1")
        attention(1, "l1")
        project(1, "l1", flat)
        dve.wait_ge(named("l1proj_add"), NT)
        normalize(4, flat, 1e-5)
        mlp()
        normalize(5, x_res, 1e-5, flat)
        gating(1, E1, FFC[2])
        routing(1, E1)
        output_bias(1)
        experts(1, "l1", E1)
        mix(1, "l1", True)

    @block.scalar
    def _(act):
        def root(k):
            act.wait_ge(named("var"), k + 1)
            act.activation(std[:, :], var_eps[:, :], ACT.Sqrt).then_inc(named("std"), 1)

        def to_xT(k, aff=None):
            if aff is not None:
                act.wait_ge(named("const"), 16)
            for t in range(NT):
                act.wait_ge(named("ln_tr"), LN_PE[k] + t + 1)
                tok = slice(t * P, (t + 1) * P)
                if aff is None:
                    ins = act.activation(xT[:, :, tok], bank[:, t % 4, 0:C].rearrange("p (c q) -> p c q", c=NC_),
                                         ACT.Copy)
                else:
                    for c in range(NC_):
                        ins = act.activation(xT[:, c, tok], bank[:, t % 4, c * P:(c + 1) * P], ACT.Identity,
                                             scale=affine[:, aff, 0, c:c + 1], bias=affine[:, aff, 1, c:c + 1])
                ins.then_inc(named("xT"), 1)

        def high_halves(n, pre):
            for t in range(NT):
                act.wait_ge(named(f"{pre}qk_tr"), t + 1)
                if t % 2 == 0 and t >= 4:
                    act.wait_ge(named(f"{pre}first{t // 2 % 2}"), 16 * 6 * (t // 4))
                    act.wait_ge(named(f"{pre}stack{t // 2 % 2}"), 16 * 18 * (t // 4))
                for i in range(2):
                    ins = act.activation(stage[:, t // 2 % 2, 2 * i, :, P * (t % 2):P * (t % 2) + P],
                                         bank[:, 6 + i, 0:C].rearrange("p (c q) -> p c q", c=NC_), ACT.Copy)
                ins.then_inc(named(f"{pre}hi"), 1)

        def softmax(n, pre):
            def keep(h, i):
                half, sums = divmod(i, 2)
                c, j = divmod(HEADS[h], HPC)
                to = den if sums else attT
                act.activation(to[D * j:D * j + D, c, half * HALF:half * HALF + HALF],
                               bank[D * i:D * i + D, 6 + (h + half) % 2, :],
                               ACT.Copy).then_inc(named(f"{pre}acc_copy"), 1)

            act.wait_ge(named(f"{pre}qkv_mm"), NT)
            for u in range(H * NT):
                h, kt = divmod(u, NT)
                act.wait_ge(named(f"{pre}st"), u + 1)
                if u >= P_RING:
                    act.wait_ge(named(f"{pre}pv"), u - P_RING + 1)
                act.activation(probs[:, u % P_RING, :], bank[:, 4:6, :].rearrange("p a b -> p (a b)"), ACT.Exp,
                               scale=SCALE).then_inc(named(f"{pre}exp"), 1)
                if h and 2 <= kt < 6:
                    act.wait_ge(named(f"{pre}pv"), NT * h)
                    keep(h - 1, kt - 2)
            act.wait_ge(named(f"{pre}pv"), NT * H)
            for i in range(4):
                keep(H - 1, i)

        def mlp_gelu():
            act.wait_ge(named("ffc"), FFC[1])
            for v in range(NH):
                for f in range(NF):
                    act.wait_ge(named("ff_h"), NF * v + f + 1)
                    act.activation(hT[:, v, f, :], bank[:, f % 4, :], ACT.Gelu,
                                   bias=b1[:, E0 + E1, f:f + 1]).then_inc(named("ff_g"), 1)

        def experts(k, pre, n_e, func, row):
            act.wait_ge(named("plan"), k + 1)
            with act.Fori(0, n_e) as e:
                n_tiles = act.value_load(plan[0:1, 0, bass.ds(e, 1)], min_val=1, max_val=EM)
                first = act.value_load(plan[0:1, 1, bass.ds(e, 1)], min_val=0, max_val=TILES - 1)
                with act.Fori(0, n_tiles) as i:
                    for f in range(NF):
                        act.wait_ge(named(f"{pre}h"), (first + i) * NF + (f + 1))
                        act.activation(hT[:, 0, f, 0:P], bank[:, f % 4, 0:P], func,
                                       bias=b1[:, bass.ds(e + row, 1), f]).then_inc(named(f"{pre}g"), 1)

        def gap(k):
            act.wait_ge(named("gap"), k + 1)
            act.activation(gates[:, 1, :], gates[:, 0, :], ACT.Exp).then_inc(named("gap_exp"), 1)

        root(0)
        to_xT(0)
        high_halves(0, "l0")
        softmax(0, "l0")
        root(1)
        to_xT(1)
        gap(0)
        experts(0, "l0", E0, ACT.Gelu_apprx_tanh, 0)
        root(2)
        root(3)
        to_xT(3, 0)
        high_halves(1, "l1")
        softmax(1, "l1")
        root(4)
        to_xT(4, 1)
        mlp_gelu()
        root(5)
        to_xT(5)
        gap(1)
        experts(1, "l1", E1, ACT.Gelu, E0)

    @block.tensor
    def _(pe):
        def transposes(k):
            pe.wait_ge(named("ident"), 1)
            for t in range(NT):
                pe.wait_ge(named("xn"), XN[k] + t + 1)
                if t >= 4:
                    pe.wait_ge(named("xT"), LN_PE[k] + t - 3)
                tile = flat[:, t, :] if k in (1, 5) else xn[:, t % 2, :]
                for c in range(NC_):
                    ins = pe.transpose(bank[:, t % 4, c * P:(c + 1) * P], tile[:, c * P:(c + 1) * P], ident[:, :])
                ins.then_inc(named("ln_tr"), 1)
            pe.wait_ge(named("xT"), LN_PE[k] + NT)

        def qkv(n, pre):
            pe.wait_ge(named(f"{pre}w"), 32)
            for t in range(NT + 1):
                if t < NT:
                    b = 3 * (t % 2)
                    if t >= 2:
                        pe.wait_ge(named(f"{pre}v"), t - 1)
                    for i in range(3):
                        for c in range(NC_):
                            ins = pe.matmul(bank[:, b + i, 0:C], xT[:, c, t * P:(t + 1) * P],
                                            w_qkv[:, c, C * i:C * i + C], start=(c == 0), stop=(c == NC_ - 1))
                    ins.then_inc(named(f"{pre}qkv_mm"), 1)
                if t:
                    u = t - 1
                    pe.wait_ge(named(f"{pre}qk"), u + 1)
                    if u:
                        pe.wait_ge(named(f"{pre}lo"), u)
                    for i in range(2):
                        for c in range(NC_):
                            ins = pe.transpose(bank[:, 6 + i, c * P:(c + 1) * P],
                                               qk_tok[:, C * i + c * P:C * i + c * P + P], ident[:, :])
                    ins.then_inc(named(f"{pre}qk_tr"), 1)
            pe.wait_ge(named(f"{pre}lo"), NT)
            pe.wait_ge(named(f"{pre}v"), NT)

        def attention(n, pre):
            order = maxima_order()
            at = [0]
            for i in range(2):
                pe.wait_ge(named(f"{pre}first{i}"), 16 * 6 * NQ // 2)
            pe.wait_ge(named("ones"), 2 * (n + 1))
            if n:
                pe.wait_ge(named("bias_of"), H)

            def maxima(count):
                for _ in range(count):
                    if at[0] == len(order):
                        return
                    kind, h, t = order[at[0]]
                    if at[0] >= 2:
                        was, h2, t2 = order[at[0] - 2]
                        if was == "tile":
                            pe.wait_ge(named(f"{pre}mx_read"), NT * h2 + t2 + 1)
                        else:
                            pe.wait_ge(named(f"{pre}shift"), h2 + 1)
                    pair = 2 * (at[0] % 2)
                    tok = slice(t * P, (t + 1) * P)
                    head = HEADS[h]
                    if kind == "tile":
                        if h == NC_ and t == 0:
                            for i in range(2):
                                pe.wait_ge(named(f"{pre}stack{i}"), 16 * 18 * NQ // 2)
                        own = t // (HALF // P)
                        for half in range(NH):
                            diag = n and half == own
                            ins = pe.matmul(bank[:, pair + half, :], q_stack[0:ROW_MAX, head, tok],
                                            k_stack[0:ROW_MAX, head, half * HALF:half * HALF + HALF],
                                            start=True, stop=not diag)
                            if diag:
                                o = t * P - own * HALF
                                ins = pe.matmul(bank[:, pair + half, o:o + P], bias_of[:, head, :], key_of[:, :],
                                                start=False, stop=True)
                    else:
                        pe.wait_ge(named(f"{pre}neg"), h + 1)
                        ins = pe.transpose(bank[0:NT, pair, 0:P], neg_max[:, h, :], ident[:, :])
                    ins.then_inc(named(f"{pre}mx_mm"), 1)
                    at[0] += 1

            def values(u):
                h, kt = divmod(u, NT)
                pe.wait_ge(named(f"{pre}exp"), u + 1)
                if kt == 0 and h >= 2:
                    pe.wait_ge(named(f"{pre}acc_copy"), 4 * (h - 1))
                head = HEADS[h]
                for half in range(NH):
                    b = 6 + (h + half) % 2
                    p = probs[:, u % P_RING, half * HALF:half * HALF + HALF]
                    o = 64 * half
                    pe.matmul(bank[o:o + D, b, :], v_tok[:, kt, D * head:D * head + D], p,
                              start=(kt == 0), stop=(kt == NT - 1))
                    ins = pe.matmul(bank[o + D:o + 2 * D, b, :], ones_v[:, :], p,
                                    start=(kt == 0), stop=(kt == NT - 1))
                ins.then_inc(named(f"{pre}pv"), 1)

            maxima(LEAD)
            for u in range(H * NT):
                h, kt = divmod(u, NT)
                head = HEADS[h]
                if kt == 0:
                    pe.wait_ge(named(f"{pre}shifted{h % 2}"), 16 * (h // 2 + 1))
                if u:
                    pe.wait_ge(named(f"{pre}exp"), u)
                own = kt // (HALF // P)
                for half in range(NH):
                    diag = n and half == own
                    ins = pe.matmul(bank[:, 4 + half, :], k_stack[0:ROW_MAX + 1, head, kt * P:(kt + 1) * P],
                                    q_stack[0:ROW_MAX + 1, head, half * HALF:half * HALF + HALF],
                                    start=True, stop=not diag)
                    if diag:
                        o = kt * P - own * HALF
                        ins = pe.matmul(bank[:, 4 + half, o:o + P], key_of[:, :], bias_of[:, head, :],
                                        start=False, stop=True)
                ins.then_inc(named(f"{pre}st"), 1)
                maxima(1 + (kt == 0))
                if u:
                    values(u - 1)
            values(H * NT - 1)

        def project(n, pre):
            pe.wait_ge(named(f"{pre}w2"), 32)
            for t in range(NT):
                pe.wait_ge(named(f"{pre}att"), NT * (NC_ - 1) + t + 1)
                if t >= 4:
                    pe.wait_ge(named(f"{pre}proj_add"), t - 3)
                for c in range(NC_):
                    ins = pe.matmul(bank[:, t % 4, 0:C], attT[:, c, t * P:(t + 1) * P], w_o[:, c, :],
                                    start=(c == 0), stop=(c == NC_ - 1))
                ins.then_inc(named(f"{pre}proj"), 1)

        def gating(k, n_e, ffc):
            pe.wait_ge(named("ffc"), ffc)
            for t in range(NT):
                if t >= 2:
                    pe.wait_ge(named("gate_top"), NT * k + t - 1)
                for c in range(NC_):
                    ins = pe.matmul(bank[:, 4 + t % 2, 0:n_e], xT[:, c, t * P:(t + 1) * P], w_gate[:, c, 0:n_e],
                                    start=(c == 0), stop=(c == NC_ - 1))
                ins.then_inc(named("gate_mm"), 1)
            pe.wait_ge(named("routed"), k + 1)
            rhs = routed[:, :, :].rearrange("p t e -> p (t e)")
            pe.matmul(bank[:, 4, 0:NT * EM], tri[:, :], rhs, start=True, stop=True)
            pe.matmul(bank[:, 5, 0:NT * EM], ones[:, :], rhs, start=True, stop=True).then_inc(named("counted"), 1)
            pe.wait_ge(named("slots"), k + 1)
            pe.wait_ge(named("comb"), k + 1)
            for t in range(NT):
                if t >= 2:
                    pe.wait_ge(named("combT"), NT * k + t - 1)
                pe.transpose(bank[0:EM, 4 + t % 2, 0:P], comb[:, t, :], ident[:, :]).then_inc(named("comb_tr"), 1)
            for t in range(NT):
                pe.wait_ge(named("combT"), NT * k + t + 1)
                if t >= 2:
                    pe.wait_ge(named("b2_add"), NT * k + t - 1)
                pe.matmul(bank[:, 6 + t % 2, 0:C], combT[0:n_e, t * P:(t + 1) * P], b2[0:n_e, :],
                          start=True, stop=True).then_inc(named("b2_mm"), 1)
            pe.wait_ge(named("b2_add"), NT * (k + 1))

        def experts(k, pre, n_e, flip):
            def turn():
                for c in range(NC_):
                    ins = pe.transpose(bank[:, 6, c * P:(c + 1) * P], x_tile[:, c * P:(c + 1) * P], ident[:, :])
                ins.then_inc(named(f"{pre}x_tr"), 1)

            pe.wait_ge(named(f"{pre}x_in"), 16)
            turn()
            pe.wait_ge(named("plan"), k + 1)
            with pe.Fori(0, n_e // 2) as pair:
                for s in range(2):
                    w1_, w2_ = w1[s ^ flip], w2[s ^ flip]
                    n_tiles = pe.value_load(plan[0:1, 0, bass.ds(pair * 2 + s, 1)], min_val=1, max_val=EM)
                    first = pe.value_load(plan[0:1, 1, bass.ds(pair * 2 + s, 1)], min_val=0, max_val=TILES - 1)
                    with pe.Fori(0, n_tiles) as i:
                        g = first + i
                        pe.wait_ge(named(f"{pre}w{s}_"), pair * 16 + 16)
                        pe.wait_ge(named(f"{pre}xT_sb"), g + 1)
                        for f in range(NF):
                            if f >= 4:
                                pe.wait_ge(named(f"{pre}g"), g * NF + (f - 3))
                            for c in range(NC_):
                                ins = pe.matmul(bank[:, f % 4, 0:P], w1_[:, c, f * P:(f + 1) * P],
                                                xT_tile[:, c, :], start=(c == 0), stop=(c == NC_ - 1))
                            ins.then_inc(named(f"{pre}h"), 1)
                        pe.wait_ge(named(f"{pre}x_in"), g * 16 + 32)
                        turn()
                        pe.wait_ge(named(f"{pre}w{s}_2"), pair * 16 + 16)
                        pe.wait_ge(named(f"{pre}y_sb"), g + 1)
                        for f in range(NF):
                            pe.wait_ge(named(f"{pre}g"), g * NF + (f + 1))
                            ins = pe.matmul(bank[:, 4, 0:C], hT[:, 0, f, 0:P], w2_[:, f, :],
                                            start=(f == 0), stop=(f == NF - 1))
                        ins.then_inc(named(f"{pre}y_mm"), 1)

        def mlp():
            pe.wait_ge(named("ffc"), FFC[1])
            pe.wait_ge(named("mlpw"), 16)

            def hidden(half):
                for f in range(NF):
                    if half or f >= 4:
                        pe.wait_ge(named("ff_g"), NF * half + f - 3)
                    for c in range(NC_):
                        ins = pe.matmul(bank[:, f % 4, :], w1[0][:, c, f * P:(f + 1) * P],
                                        xT[:, c, half * HALF:half * HALF + HALF], start=(c == 0), stop=(c == NC_ - 1))
                    ins.then_inc(named("ff_h"), 1)

            def outputs(half):
                for i in range(NT // NH):
                    t = NT // NH * half + i
                    if t >= 2:
                        pe.wait_ge(named("ff_add"), t - 1)
                    pe.matmul(bank[:, 4 + t % 2, 0:C], ones_row[:, :], b2[0:1, :], start=True, stop=False)
                    for f in range(NF):
                        if i == 0:
                            pe.wait_ge(named("ff_g"), NF * half + f + 1)
                        ins = pe.matmul(bank[:, 4 + t % 2, 0:C], hT[:, half, f, i * P:(i + 1) * P],
                                        w2[0][:, f, :], start=False, stop=(f == NF - 1))
                    ins.then_inc(named("ff_y"), 1)

            hidden(0)
            hidden(1)
            pe.wait_ge(named("mlpw2"), 16)
            outputs(0)
            outputs(1)

        transposes(0)
        qkv(0, "l0")
        attention(0, "l0")
        project(0, "l0")
        transposes(1)
        gating(0, E0, FFC[0])
        experts(0, "l0", E0, 0)
        transposes(3)
        qkv(1, "l1")
        attention(1, "l1")
        project(1, "l1")
        transposes(4)
        mlp()
        transposes(5)
        gating(1, E1, FFC[2])
        experts(1, "l1", E1, 1)


def kernel(**inputs):
    import concourse.bacc as bacc
    from concourse.bass_utils import run_bass_kernel_spmd

    i = {k: np.asarray(v) for k, v in inputs.items()}

    def turned(w):
        return np.ascontiguousarray(np.swapaxes(w, -1, -2))

    def by_channel(v, n):
        return np.ascontiguousarray(np.moveaxis(v.reshape(v.shape[:-1] + (n, P)), -1, 0))

    half = D // 2
    pair = np.arange(ROPE, dtype=np.float32)
    angles = np.arange(T, dtype=np.float32)[:, None] / (np.float32(10000.0) ** (np.float32(2.0) * pair / np.float32(D)))
    trig = np.stack([np.cos(angles), np.sin(angles)]).astype(np.float32).reshape(2, NT, P, ROPE).transpose(2, 0, 1, 3)

    arrays = {
        "x": i["x"].reshape(T, C),
        "trig": trig,
        "affine": np.stack([by_channel(np.stack([i["L1_conv_ln1_g"], i["L1_conv_ln1_b"]]), NC_),
                            by_channel(np.stack([i["L1_conv_ln3_g"], i["L1_conv_ln3_b"]]), NC_)], axis=1),
        "l0qkv": turned(i["L0_conv_qkv_w"]), "l0bqkv": i["L0_conv_qkv_b"],
        "l0wo": turned(i["L0_conv_proj_w"]), "l0bo": i["L0_conv_proj_b"],
        "l0gate_w": turned(i["L0_ffn_gate_w"]), "l0gate_b": i["L0_ffn_gate_b"],
        "l0w1": turned(i["L0_ffn_w_fc"]), "l0w2": turned(i["L0_ffn_w_proj"]), "l0b2": i["L0_ffn_b_proj"],
        "b1": by_channel(np.concatenate([i["L0_ffn_b_fc"], i["L1_ffn_b1"], i["L1_conv_b1"][None]]), NF),
        "l1qkv": np.concatenate([i["L1_conv_wq"], i["L1_conv_wk"], i["L1_conv_wv"]], axis=1),
        "l1bqkv": np.concatenate([i["L1_conv_bq"], i["L1_conv_bk"], i["L1_conv_bv"]]),
        "l1wo": i["L1_conv_wo"], "l1bo": i["L1_conv_bo"],
        "attn_biases": turned(i["L1_conv_attn_biases"]),
        "mlp_w1": i["L1_conv_w1"], "mlp_w2": i["L1_conv_w2"], "mlp_b2": i["L1_conv_b2"][None],
        "l1gate_w": i["L1_ffn_gate_w"], "l1gate_b": i["L1_ffn_gate_b"],
        "l1w1": i["L1_ffn_w1"], "l1w2": i["L1_ffn_w2"], "l1b2": i["L1_ffn_b2"],
    }
    nc = bacc.Bacc("TRN2", target_bir_lowering=False, num_devices=1)
    arrays = {f"in_{k}": np.ascontiguousarray(v) for k, v in arrays.items()}
    aps = {k[3:]: nc.dram_tensor(k, v.shape, mybir.dt.from_np(v.dtype), kind="ExternalInput").ap()
           for k, v in arrays.items()}
    out = nc.dram_tensor("out_x", (T, C), F32, kind="ExternalOutput").ap()
    build(nc, aps, out)
    r = run_bass_kernel_spmd(nc, [arrays], core_ids=[0])
    return r.results[0]["out_x"].reshape(1, 32, 32, C)
```
